# Optimizing a Trainium2 kernel written in Bass

```python
import numpy as np
import jax
import jax.numpy as jnp

def _softmax(x, axis=-1):
    return jax.nn.softmax(x, axis=axis)

def _gelu(x):
    return jax.nn.gelu(x, approximate=True)

def _silu(x):
    return jax.nn.silu(x)

def _sigmoid(x):
    return jax.nn.sigmoid(x)

def _layernorm(x, axis=-1, eps=1e-05):
    m = jnp.mean(x, axis=axis, keepdims=True)
    v = jnp.var(x, axis=axis, keepdims=True)
    return (x - m) / jnp.sqrt(v + eps)

def _scatter_add(tgt, idx, src, axis=0):
    return tgt.at[idx].add(src)

def _segment_sum(src, seg, n):
    return jax.ops.segment_sum(src, seg, n)
kernel_name = 'mk_gnn_resnorm_d1_gnn_r32_0fb87e'

def setup_inputs(seed: int=0):
    np.random.seed(seed)
    _w = jnp.asarray

    def _rec_inputs():
        import jax
        import jax.numpy as jnp
        _gk = jax.random.key(seed)
        x = -0.0008691 + 1 * jax.random.normal(jax.random.fold_in(_gk, 1), (3125, 64), jnp.float32)
        _s = jax.random.randint(jax.random.fold_in(_gk, 2), (50000,), 0, 3125, jnp.int32)
        _d = jax.random.randint(jax.random.fold_in(_gk, 3), (50000,), 0, 3125, jnp.int32)
        _loop = jnp.arange(3125, dtype=jnp.int32)
        src = jnp.concatenate([_s, _d, _loop])
        dst = jnp.concatenate([_d, _s, _loop])
        _o = jnp.argsort(dst, stable=True)
        src = src[_o]
        dst = dst[_o]
        return (x, src, dst)
    x, src, dst = _rec_inputs()

    def _L0_gnn_setup():
        import jax, jax.numpy as jnp
        import numpy as np
        N = 625
        E = 10000
        F = 64
        H = 4
        G = 32
        EPS = 1e-05

        def _gatv2(x, src, dst, Wl, bl, Wr, br, att, bias):
            n = x.shape[0]
            h, c = att.shape
            xl = (x @ Wl + bl).reshape(n, h, c)
            xr = (x @ Wr + br).reshape(n, h, c)
            e = jax.nn.leaky_relu(xl[src] + xr[dst], 0.2)
            s = jnp.einsum('ehc,hc->eh', e, att)
            m = jax.ops.segment_max(s, dst, num_segments=n)
            a = jnp.exp(s - m[dst])
            alpha = a / jax.ops.segment_sum(a, dst, num_segments=n)[dst]
            out = jax.ops.segment_sum(alpha[:, :, None] * xl[src], dst, num_segments=n)
            return out.reshape(n, h * c) + bias
        key = jax.random.key(seed)
        ks = jax.random.split(key, 20)
        d = {}
        d['x'] = jax.random.normal(ks[0], (N, F), jnp.float32)
        d['edge_index'] = jax.random.randint(ks[1], (2, E), 0, N)
        d['batch'] = jnp.sort(jax.random.randint(ks[2], (N,), 0, G))
        layer_cfg = [('l0', F, H), ('l1', F * H, H), ('l2', F * H, H), ('l3', F * H, 1)]
        i = 3
        for name, ic, h in layer_cfg:
            kk = jax.random.split(ks[i], 3)
            i += 1
            scale = 1.0 / np.sqrt(ic)
            d[name + '_Wl'] = jax.random.normal(kk[0], (ic, h * F), jnp.float32) * scale
            d[name + '_bl'] = jnp.zeros((h * F,), jnp.float32)
            d[name + '_Wr'] = jax.random.normal(kk[1], (ic, h * F), jnp.float32) * scale
            d[name + '_br'] = jnp.zeros((h * F,), jnp.float32)
            d[name + '_att'] = jax.random.normal(kk[2], (h, F), jnp.float32) * (1.0 / np.sqrt(F))
            d[name + '_bias'] = jnp.zeros((h * F,), jnp.float32)
        d['ln_w'] = jnp.ones((F,), jnp.float32)
        d['ln_b'] = jnp.zeros((F,), jnp.float32)
        return d
    _L0_gnn_all = _L0_gnn_setup()
    _L0_gnn_in = {k: v for k, v in _L0_gnn_all.items() if k in ('l0_Wl', 'l0_bl', 'l0_Wr', 'l0_br', 'l0_att', 'l0_bias', 'l1_Wl', 'l1_bl', 'l1_Wr', 'l1_br', 'l1_att', 'l1_bias', 'l2_Wl', 'l2_bl', 'l2_Wr', 'l2_br', 'l2_att', 'l2_bias', 'l3_Wl', 'l3_bl', 'l3_Wr', 'l3_br', 'l3_att', 'l3_bias', 'ln_w', 'ln_b')}
    del _L0_gnn_all
    return {'x': x, 'src': src, 'dst': dst, 'L0_gnn_l0_Wl': _L0_gnn_in['l0_Wl'], 'L0_gnn_l0_bl': _L0_gnn_in['l0_bl'], 'L0_gnn_l0_Wr': _L0_gnn_in['l0_Wr'], 'L0_gnn_l0_br': _L0_gnn_in['l0_br'], 'L0_gnn_l0_att': _L0_gnn_in['l0_att'], 'L0_gnn_l0_bias': _L0_gnn_in['l0_bias'], 'L0_gnn_l1_Wl': _L0_gnn_in['l1_Wl'], 'L0_gnn_l1_bl': _L0_gnn_in['l1_bl'], 'L0_gnn_l1_Wr': _L0_gnn_in['l1_Wr'], 'L0_gnn_l1_br': _L0_gnn_in['l1_br'], 'L0_gnn_l1_att': _L0_gnn_in['l1_att'], 'L0_gnn_l1_bias': _L0_gnn_in['l1_bias'], 'L0_gnn_l2_Wl': _L0_gnn_in['l2_Wl'], 'L0_gnn_l2_bl': _L0_gnn_in['l2_bl'], 'L0_gnn_l2_Wr': _L0_gnn_in['l2_Wr'], 'L0_gnn_l2_br': _L0_gnn_in['l2_br'], 'L0_gnn_l2_att': _L0_gnn_in['l2_att'], 'L0_gnn_l2_bias': _L0_gnn_in['l2_bias'], 'L0_gnn_l3_Wl': _L0_gnn_in['l3_Wl'], 'L0_gnn_l3_bl': _L0_gnn_in['l3_bl'], 'L0_gnn_l3_Wr': _L0_gnn_in['l3_Wr'], 'L0_gnn_l3_br': _L0_gnn_in['l3_br'], 'L0_gnn_l3_att': _L0_gnn_in['l3_att'], 'L0_gnn_l3_bias': _L0_gnn_in['l3_bias'], 'L0_gnn_ln_w': _L0_gnn_in['ln_w'], 'L0_gnn_ln_b': _L0_gnn_in['ln_b']}

def reference(x, src, dst, L0_gnn_l0_Wl, L0_gnn_l0_bl, L0_gnn_l0_Wr, L0_gnn_l0_br, L0_gnn_l0_att, L0_gnn_l0_bias, L0_gnn_l1_Wl, L0_gnn_l1_bl, L0_gnn_l1_Wr, L0_gnn_l1_br, L0_gnn_l1_att, L0_gnn_l1_bias, L0_gnn_l2_Wl, L0_gnn_l2_bl, L0_gnn_l2_Wr, L0_gnn_l2_br, L0_gnn_l2_att, L0_gnn_l2_bias, L0_gnn_l3_Wl, L0_gnn_l3_bl, L0_gnn_l3_Wr, L0_gnn_l3_br, L0_gnn_l3_att, L0_gnn_l3_bias, L0_gnn_ln_w, L0_gnn_ln_b):
    import jax
    import jax.numpy as jnp

    def _L0_gnn_ref(x, edge_index, batch, l0_Wl, l0_bl, l0_Wr, l0_br, l0_att, l0_bias, l1_Wl, l1_bl, l1_Wr, l1_br, l1_att, l1_bias, l2_Wl, l2_bl, l2_Wr, l2_br, l2_att, l2_bias, l3_Wl, l3_bl, l3_Wr, l3_br, l3_att, l3_bias, ln_w, ln_b):
        import jax, jax.numpy as jnp
        import numpy as np
        N = 625
        E = 10000
        F = 64
        H = 4
        G = 32
        EPS = 1e-05

        def _gatv2(x, src, dst, Wl, bl, Wr, br, att, bias):
            n = x.shape[0]
            h, c = att.shape
            xl = (x @ Wl + bl).reshape(n, h, c)
            xr = (x @ Wr + br).reshape(n, h, c)
            e = jax.nn.leaky_relu(xl[src] + xr[dst], 0.2)
            s = jnp.einsum('ehc,hc->eh', e, att)
            m = jax.ops.segment_max(s, dst, num_segments=n)
            a = jnp.exp(s - m[dst])
            alpha = a / jax.ops.segment_sum(a, dst, num_segments=n)[dst]
            out = jax.ops.segment_sum(alpha[:, :, None] * xl[src], dst, num_segments=n)
            return out.reshape(n, h * c) + bias
        n = x.shape[0]
        loop = jnp.arange(n)
        src = jnp.concatenate([edge_index[0], loop])
        dst = jnp.concatenate([edge_index[1], loop])
        lrelu = lambda t: jax.nn.leaky_relu(t, 0.01)
        h = lrelu(_gatv2(x, src, dst, l0_Wl, l0_bl, l0_Wr, l0_br, l0_att, l0_bias))
        h = lrelu(_gatv2(h, src, dst, l1_Wl, l1_bl, l1_Wr, l1_br, l1_att, l1_bias))
        h = lrelu(_gatv2(h, src, dst, l2_Wl, l2_bl, l2_Wr, l2_br, l2_att, l2_bias))
        h = lrelu(_gatv2(h, src, dst, l3_Wl, l3_bl, l3_Wr, l3_br, l3_att, l3_bias)) + x
        cnt = jax.ops.segment_sum(jnp.ones((n,), h.dtype), batch, num_segments=G) * h.shape[1]
        mean = jax.ops.segment_sum(h.sum(-1), batch, num_segments=G) / cnt
        hc = h - mean[batch][:, None]
        var = jax.ops.segment_sum((hc * hc).sum(-1), batch, num_segments=G) / cnt
        return hc / jnp.sqrt(var + EPS)[batch][:, None] * ln_w + ln_b
    edge_index = jnp.stack([src, dst])
    batch0 = jnp.zeros((3125,), jnp.int32)
    x = _layernorm(x + _L0_gnn_ref(x, edge_index, batch0, L0_gnn_l0_Wl, L0_gnn_l0_bl, L0_gnn_l0_Wr, L0_gnn_l0_br, L0_gnn_l0_att, L0_gnn_l0_bias, L0_gnn_l1_Wl, L0_gnn_l1_bl, L0_gnn_l1_Wr, L0_gnn_l1_br, L0_gnn_l1_att, L0_gnn_l1_bias, L0_gnn_l2_Wl, L0_gnn_l2_bl, L0_gnn_l2_Wr, L0_gnn_l2_br, L0_gnn_l2_att, L0_gnn_l2_bias, L0_gnn_l3_Wl, L0_gnn_l3_bl, L0_gnn_l3_Wr, L0_gnn_l3_br, L0_gnn_l3_att, L0_gnn_l3_bias, L0_gnn_ln_w, L0_gnn_ln_b), axis=-1)
    return x

_drawn_inputs = setup_inputs


def setup_inputs(seed=0):
    import zlib

    import numpy as np

    out = dict(_drawn_inputs(seed))
    spreads = {'L0_gnn_l0_bl': (0.0, 0.8),
     'L0_gnn_l0_br': (0.0, 0.8),
     'L0_gnn_l0_bias': (0.0, 0.8),
     'L0_gnn_l1_bl': (0.0, 0.506),
     'L0_gnn_l1_br': (0.0, 0.8),
     'L0_gnn_l1_bias': (0.0, 0.525),
     'L0_gnn_l2_bl': (0.0, 0.338),
     'L0_gnn_l2_br': (0.0, 0.8),
     'L0_gnn_l2_bias': (0.0, 0.415),
     'L0_gnn_l3_bl': (0.0, 0.8),
     'L0_gnn_l3_br': (0.0, 0.8),
     'L0_gnn_l3_bias': (0.0, 0.8),
     'L0_gnn_ln_w': (1.0, 0.2),
     'L0_gnn_ln_b': (0.0, 0.1)}
    factors = {'L0_gnn_l0_Wl': 8.0,
     'L0_gnn_l0_Wr': 8.0,
     'L0_gnn_l0_att': 6.821,
     'L0_gnn_l1_Wl': 3.473,
     'L0_gnn_l1_Wr': 8.0,
     'L0_gnn_l1_att': 8.0,
     'L0_gnn_l2_Wr': 8.0,
     'L0_gnn_l2_att': 8.0,
     'L0_gnn_l3_Wr': 8.0,
     'L0_gnn_l3_att': 8.0}
    for name, (base, spread) in spreads.items():
        noise = np.random.default_rng([zlib.crc32(name.encode()), seed]).standard_normal(out[name].shape)
        drawn = base * np.exp(spread * noise) if base else spread * noise
        out[name] = jnp.asarray(drawn.astype(out[name].dtype))
    for name, factor in factors.items():
        out[name] = (out[name] * factor).astype(out[name].dtype)
    return out
```

```python
from contextlib import ExitStack

import concourse.bass as bass
from concourse import mybir

F32 = mybir.dt.float32
BF16 = mybir.dt.bfloat16
I32 = mybir.dt.int32
ALU = mybir.AluOpType
ACT = mybir.ActivationFunctionType
AX = mybir.AxisListType

P = 128
CT = 32
GT = 4
NG = CT // GT
HMAX = 4
LAG = NG + 5
BIG = 2.0 ** 100
SLOPE_ATT = 0.2
SLOPE_OUT = 0.01
EPS = 1e-5
PARTS = 3

SV = 18
SP_ = 4
SA = 4


def ceil_div(a, b):
    return -(-a // b)


def lin(c, a, b):
    i, k = c
    return a * k + b if i is None else i * (2 * a) + (a * k + b)


def shift(c, d):
    return (c[0], c[1] + d)


def program(nc, x, src, dst, layers, ln_w, ln_b, out):
    N, F = x.shape
    E = src.shape[0]
    NB = ceil_div(N, P)
    OT = ceil_div(E, P)
    NC = ceil_div(OT + NB - 1, CT)
    NC += NC % 2
    NT = NC * CT
    TG = ceil_div(NT, P)
    NL = len(layers)
    HS = [lay["att"].shape[0] for lay in layers]
    FS = [h * F for h in HS]
    FP = [max(f, P) for f in FS]
    WR = [FP[l] + HS[l] for l in range(NL)]
    WS = [FS[l] + 2 * HS[l] for l in range(NL)]
    KI = [F] + FS[:-1]
    KC = [ceil_div(k, P) for k in KI]
    KP = [min(k, P) for k in KI]
    WROW, WSUM, FMAX = max(WR), max(WS), max(FS)
    AREA = NB * WROW
    EDIV = max(d for d in range(1, P + 1) if E % d == 0)
    EROW = E // EDIV
    LASTN = N - (NB - 1) * P
    NPAD = (OT + 1) * P - E
    W_DMAS = [0]
    for l in range(NL):
        W_DMAS.append(W_DMAS[-1] + 16 * (2 * KC[l] + 4 + HS[l]))
    W_DMAS = W_DMAS[1:]

    with ExitStack() as ctx:
        def sb(name, shape, dt=F32):
            return ctx.enter_context(nc.sbuf_tensor(name, shape, dt))

        def sem(name):
            return ctx.enter_context(nc.semaphore(name))

        def dram(name, shape, dt=F32):
            return nc.dram_tensor(name, shape, dt, kind="Internal").ap()

        dst_d = dram("dst_padded", (OT + 1, P), I32)
        src_d = dram("src_padded", (OT + 1, P), I32)
        loc_d = dram("loc_rows", (TG * P, P), BF16)
        key_d = dram("key_rows", ((TG * P + 2) * P,))
        blk_d = dram("block_of_tile", (TG * P,), I32)
        table = [dram(f"table{l}", (NB * P, WR[l])) for l in range(NL)]

        ring = sb("ring", [P, 2 * CT * WROW])
        acc = sb("acc", [P, NB, WSUM])
        xr_parts = sb("xr_parts", [P, PARTS, NB, FMAX], BF16)
        s_self = sb("s_self", [P, NB, HMAX])
        ident = sb("ident", [P, P])
        iota_row = sb("iota_row", [P, P])
        iota_col = sb("iota_col", [P, 1])
        tile_no = sb("tile_no", [P, TG])
        block_edge = sb("block_edge", [P, NB - 1])
        ones = sb("ones", [P, P])
        pads = sb("pads", [1, 2, NPAD], I32)
        fpad = sb("fpad", [1, P])
        loc_e = sb("loc_e", [P, TG * P])
        src_e = sb("src_e", [P, TG * P], I32)
        block_row = sb("block_row", [1, NT], I32)
        pen_f = sb("pen_f", [P, NC, P], BF16)
        pen_b = sb("pen_b", [P, NC, P], BF16)
        chunk_cont = sb("chunk_cont", [1, NC])
        row_pen_f = sb("row_pen_f", [1, NC, CT], BF16)
        row_pen_b = sb("row_pen_b", [1, NC, CT], BF16)
        heads_pen_f = sb("heads_pen_f", [1, HMAX, CT + 1])
        heads_pen_b = sb("heads_pen_b", [1, HMAX, CT])
        carry_pen_f = sb("carry_pen_f", [1, NC, CT], BF16)
        carry_pen_b = sb("carry_pen_b", [1, NC, CT], BF16)
        idx = sb("idx", [P, 2, CT], I32)
        locbc = sb("locbc", [P, 2, 2 * GT * P], BF16)
        oht = sb("oht", [P, 2, 2 * GT * P], BF16)
        oh = sb("oh", [P, 2, GT, P])
        relu_z = sb("relu_z", [P, 2, GT, 2, P])
        weighted = sb("weighted", [P, 2, GT, WSUM])
        score = sb("score", [P, P])
        run_fwd = sb("run_fwd", [P, P])
        run_bwd = sb("run_bwd", [P, P])
        edge_max = sb("edge_max", [P, P])
        shifted = sb("shifted", [P, P])
        max_last = sb("max_last", [P, P])
        prob_t = sb("prob_t", [P, P])
        prob_e = sb("prob_e", [P, 2, CT, HMAX])
        max_e = sb("max_e", [P, 2, CT, HMAX])
        run_in = sb("run_in", [1, HMAX, CT + 1])
        run_row = sb("run_row", [1, HMAX, CT + 1])
        back_row = sb("back_row", [1, HMAX, CT])
        carry_f = sb("carry_f", [1, HMAX, CT])
        carry_b = sb("carry_b", [1, HMAX, CT])
        boundary = sb("boundary", [1, 2, HMAX])
        first_hot = sb("first_hot", [1, P])
        carry_col = sb("carry_col", [P, 2 + HMAX])
        rescale = sb("rescale", [P, HMAX])
        bias_out = sb("bias_out", [P, FMAX])
        att_hi = sb("att_hi", [P, FMAX])
        att_lo = sb("att_lo", [P, FMAX])
        att_bd = sb("att_bd", [P, 2, HMAX])
        node_mask = sb("node_mask", [P, NB])
        lnw = sb("lnw", [P, 2, F])
        tiny = sb("tiny", [P, 8])

        ps_z = ctx.enter_context(nc.psum_tensor("ps_z", [P, 2, 2, 512], F32))
        ps_s = ctx.enter_context(nc.psum_tensor("ps_s", [P, 2, 256], F32))
        ps_m = ctx.enter_context(nc.psum_tensor("ps_m", [P, 512], F32))
        ps_o = ctx.enter_context(nc.psum_tensor("ps_o", [P, 2, 512], F32))
        weights = oh[:, :, :, :].rearrange("p a t n -> p a (t n)")
        tmp = relu_z[:, :, :, :, :].rearrange("p a t k e -> p (a t k e)")[:, 0:4 * FMAX].rearrange("p (k f) -> p k f", k=4)
        spare = weighted[:, :, :, :].rearrange("p a t w -> p (a t w)")
        bias_in = spare[:, 0:2 * FMAX]
        small = spare[:, 2 * FMAX:2 * FMAX + 8 * NB * HMAX].rearrange("p (k n) -> p k n", k=8)

        PM_T, PM_L, PM_F, PM_C, PM_B = 0, P, 2 * P, 3 * P, 3 * P + 2
        PM_PROB, PM_MAX = PM_L, PM_F

        dst_in = sem("dst_in")
        padded = sem("padded")
        const_ready = sem("const_ready")
        pool_own = sem("pool_own")
        dve_own = sem("dve_own")
        counts_ready = sem("counts_ready")
        counts_sum = sem("counts_sum")
        runs_ready = sem("runs_ready")
        rows_in = sem("rows_in")
        keys_ready = sem("keys_ready")
        prep_turned = sem("prep_turned")
        prep_taken = sem("prep_taken")
        stored = sem("stored")
        keys_in = sem("keys_in")
        lists_ready = sem("lists_ready")
        x_room = sem("x_room")
        x_in = sem("x_in")
        att_room = sem("att_room")
        weights_in = sem("weights_in")
        att_ready = sem("att_ready")
        h_ready = sem("h_ready")
        turned = sem("turned")
        turned_out = sem("turned_out")
        projected = sem("projected")
        taken = sem("taken")
        table_ready = sem("table_ready")
        table_out = sem("table_out")
        table_again = sem("table_again")
        merge_ready = sem("merge_ready")
        merge_exp = sem("merge_exp")
        stat_ready = sem("stat_ready")
        stat_sum = sem("stat_sum")
        x_again_room = sem("x_again_room")
        root_go = sem("root_go")
        root_done = sem("root_done")
        result_ready = sem("result_ready")
        result_out = sem("result_out")
        gathered = [sem(f"gathered{j}") for j in range(2 * NG)]
        idx_ready = sem("idx_ready")
        pool_go = sem("pool_go")
        loc_in = [sem(f"loc_in{j}") for j in range(2)]
        oht_ready = sem("oht_ready")
        z_ready = sem("z_ready")
        relu_ready = sem("relu_ready")
        scored = sem("scored")
        sm_v = sem("sm_v")
        sm_p = sem("sm_p")
        sm_a = sem("sm_a")
        row_pen = sem("row_pen")
        prepared = sem("prepared")
        columns = sem("columns")
        summed = sem("summed")
        flushed = sem("flushed")
        rescaled = sem("rescaled")

        block = ctx.enter_context(nc.Block())

        def area(which, width):
            o = which * AREA
            return ring[:, o:o + NB * width].rearrange("p (b f) -> p b f", b=NB)

        def turned_in(l):
            return ring[:, AREA:AREA + KC[l] * NB * P].rearrange("p (k n) -> p k n", k=KC[l])

        x_place = acc[:, :, 0:F]

        def prep(o, n, dt=F32):
            v = ring[:, o:o + n]
            return v if dt == F32 else v.bitcast(dt)

        TP = TG * P
        dst_l, dst_f, junk = prep(0, EROW, I32), prep(EROW, EROW), prep(2 * EROW, EROW)
        PR = 3 * EROW
        dst_r, src_r = prep(PR, TP, I32), prep(PR + TP, TP, I32)
        loc_w, valid, key_w, src_w = (prep(PR + k * TP, TP) for k in (2, 3, 4, 5))
        loc_bf = ring[:, PR + 6 * TP:PR + 6 * TP + TP // 2].bitcast(BF16)
        o = PR + 7 * TP
        ge, ged = prep(o, TG * (NB - 1)), prep(o + TG * (NB - 1), TG * (NB - 1))
        o += 2 * TG * (NB - 1)
        cnt, cnt_all, cmod, cdelta, cfloor, czero = (prep(o + k * (NB - 1), NB - 1) for k in range(6))
        o += 6 * (NB - 1)
        cint = prep(o, NB - 1, I32)
        o += NB - 1
        blk_f, run_f, blk128 = (prep(o + k * TG, TG) for k in range(3))
        o += 3 * TG
        blk_i, run_i = prep(o, TG, I32), prep(o + TG, TG, I32)
        key_t = [ring[:, k * NC * P:(k + 1) * NC * P].rearrange("p (c e) -> p c e", c=NC) for k in range(3)]
        o = 3 * NC * P
        first_key, last_key = ring[0:1, o:o + NT + 1], ring[0:1, o + NT + 1:o + 2 * (NT + 1)]
        o += 2 * (NT + 1)
        joined, cont = ring[0:1, o:o + NT], ring[0:1, o + NT:o + 2 * NT + 1]

        def rows(l, x2, t, n):
            s = (x2 * CT + t) * WR[l]
            return ring[:, s:s + n * WR[l]].rearrange("p (t w) -> p t w", t=n)

        def slots(c, old, new):
            def due(g):
                if g < LAG - NG:
                    return (shift(c, -2), g + 2 * NG - LAG) if old else None
                return (shift(c, -1), g + NG - LAG) if new else None
            return [(g, due(g), due(g + 1)) for g in range(NG)]

        def edge_phase(eng, l, run):
            b = l * NC
            for c, scores, softmax, old, new in ((b, True, False, False, False), (b + 1, True, True, False, True)):
                run((None, c), scores, softmax, slots((None, c), old, new))
            with eng.Fori(0, NC // 2 - 1) as i:
                for k in (2, 3):
                    run((i, b + k), True, True, slots((i, b + k), True, True))
            for c, scores, softmax, old, new in ((b + NC, False, True, True, True), (b + NC + 1, False, False, True, False)):
                run((None, c), scores, softmax, slots((None, c), old, new))

        def block_of(eng, l, c, t):
            return eng.value_load(block_row[0:1, bass.ds(local(l, c, CT, t), 1)], min_val=0, max_val=NB - 1)

        def y_root(q):
            return tiny[:, 6:7] if q == 0 else small[:, 4, 0:NB]

        def par(c):
            return c[1] % 2

        def local(l, c, a, b):
            return lin(shift(c, -l * NC), a, b)

        def at_least(eng, s, value):
            if not isinstance(value, int) or value > 0:
                eng.wait_ge(s, value)

        def broadcast(v):
            return v.rearrange("(o f) -> o f", o=1).partition_broadcast(P)[:, 0, :]

        @block.sync
        def _(sp):
            sp.dma_start(dst_l[0:EDIV, :], dst.rearrange("(p e) -> p e", p=EDIV)).then_inc(dst_in, 16)
            full = E // P * P
            n_pad = 0
            sp.wait_ge(const_ready, 1)
            for a, v, k in ((dst_d, dst, 0), (src_d, src, 1)):
                flat = a.rearrange("r e -> (r e)")
                sp.dma_start(a[0:E // P, :], v[0:full].rearrange("(r e) -> r e", e=P)).then_inc(padded, 16)
                if E > full:
                    sp.dma_start(flat[full:E].rearrange("(r e) -> r e", r=1),
                                 v[full:E].rearrange("(r e) -> r e", r=1)).then_inc(padded, 16)
                    n_pad += 1
                sp.dma_start(flat[E:E + NPAD].rearrange("(r e) -> r e", r=1), pads[0:1, k, :]).then_inc(padded, 16)
            for a in (0, (TG * P + 1) * P):
                sp.dma_start(key_d[a:a + P].rearrange("(r e) -> r e", r=1), fpad[0:1, :]).then_inc(stored, 16)
            with nc.allow_non_contiguous_dma(reason="one word per tile, once"):
                sp.wait_ge(keys_ready, 1)
                sp.dma_start(key_d[P:(TG * P + 1) * P].rearrange("(g p e) -> p g e", p=P, e=P),
                             key_w.rearrange("p (g e) -> p g e", g=TG)).then_inc(stored, 16)
                sp.dma_start(loc_d.rearrange("(g p) e -> p g e", p=P),
                             loc_bf.rearrange("p (g e) -> p g e", g=TG)).then_inc(stored, 16)
                sp.dma_start(blk_d.rearrange("(g p) -> p g", p=P), blk_i).then_inc(stored, 16)
                sp.wait_ge(stored, 5 * 16)
                sp.wait_ge(prep_taken, 1)
                sp.dma_start(block_row[:, :], blk_d[0:NT].rearrange("(o t) -> o t", o=1)).then_inc(keys_in, 16)
                for j, s in enumerate((0, -1, 1)):
                    view = key_d[P + s:P + s + NT * P].rearrange("(c t e) -> t c e", t=CT, e=P)
                    for h in range(HMAX):
                        sp.dma_start(key_t[j][h * CT:(h + 1) * CT, :, :], view).then_inc(keys_in, 16)
                sp.dma_start(first_key, key_d[P:(NT + 2) * P].rearrange("(o t e) -> o t e", o=1, e=P)[:, :, 0]).then_inc(keys_in, 16)
                sp.dma_start(last_key, key_d[0:(NT + 1) * P].rearrange("(o t e) -> o t e", o=1, e=P)[:, :, P - 1]).then_inc(keys_in, 16)

            sp.wait_ge(x_room, 1)
            sp.dma_start(x_place[:, 0:NB - 1, :], x[0:(NB - 1) * P, :].rearrange("(b p) f -> p b f", p=P)).then_inc(x_in, 16)
            sp.dma_start(x_place[0:LASTN, NB - 1, :], x[(NB - 1) * P:N, :]).then_inc(x_in, 16)

            def load_weights(l):
                lay = layers[l]
                sp.wait_ge(att_room, l + 1)
                for q, name in enumerate(("Wl", "Wr")):
                    for k in range(KC[l]):
                        sp.dma_start(weights[0:KP[l], k, q * FS[l]:(q + 1) * FS[l]],
                                     lay[name][k * P:k * P + KP[l], :]).then_inc(weights_in, 16)
                for q, name in enumerate(("bl", "br")):
                    sp.dma_start(bias_in[:, q * FS[l]:(q + 1) * FS[l]], broadcast(lay[name])).then_inc(weights_in, 16)
                sp.dma_start(bias_out[:, 0:FS[l]], broadcast(lay["bias"])).then_inc(weights_in, 16)
                sp.dma_start(att_hi[:, 0:FS[l]], broadcast(lay["att"].rearrange("h f -> (h f)"))).then_inc(weights_in, 16)
                with nc.allow_non_contiguous_dma(reason="a column of attention weights"):
                    for h in range(HS[l]):
                        a = h * F % P
                        sp.dma_start(att_bd[a:a + F, h * F // P, h:h + 1],
                                     lay["att"][h, :].rearrange("(f o) -> f o", o=1)).then_inc(weights_in, 16)

            def local_destinations(l, c, j):
                at_least(sp, oht_ready, lin(c, NG // 2, j - 1))
                sp.dma_start(locbc[:, j % 2, :],
                             loc_d[bass.ds(local(l, c, CT, j * 2 * GT), 2 * GT), :]
                             .rearrange("t e -> (t e)").rearrange("(o f) -> o f", o=1).partition_broadcast(P)[:, 0, :]
                             ).then_inc(loc_in[j % 2], 16)

            for l in range(NL):
                load_weights(l)
                sp.wait_ge(table_ready, l + 1)
                sp.dma_start(table[l].rearrange("(b p) f -> p b f", p=P), area(0, WR[l])).then_inc(table_out, 16)
                for c in range(2):
                    for j in range(NG // 2):
                        local_destinations(l, (None, l * NC + c), j)
                with sp.Fori(0, NC // 2 - 1) as i:
                    for k in (2, 3):
                        for j in range(NG // 2):
                            local_destinations(l, (i, l * NC + k), j)
                sp.wait_ge(prepared, (l + 1) * NC * NG)
                sp.dma_start(area(1, WR[l]), table[l].rearrange("(b p) f -> p b f", p=P)).then_inc(table_again, 16)
            sp.wait_ge(x_again_room, 1)
            sp.dma_start(x_place[:, 0:NB - 1, :], x[0:(NB - 1) * P, :].rearrange("(b p) f -> p b f", p=P)).then_inc(x_in, 16)
            sp.dma_start(x_place[0:LASTN, NB - 1, :], x[(NB - 1) * P:N, :]).then_inc(x_in, 16)
            sp.dma_start(lnw[:, 0, :], broadcast(ln_w)).then_inc(x_in, 16)
            sp.dma_start(lnw[:, 1, :], broadcast(ln_b)).then_inc(x_in, 16)
            sp.wait_ge(result_ready, 1)
            sp.dma_start(out[0:(NB - 1) * P, :].rearrange("(b p) f -> p b f", p=P),
                         area(0, F)[:, 0:NB - 1, :]).then_inc(result_out, 16)
            sp.dma_start(out[(NB - 1) * P:N, :], area(0, F)[0:LASTN, NB - 1, :]).then_inc(result_out, 16)
            sp.wait_ge(result_out, 32)

        @block.gpsimd
        def _(pool):
            n = [0]

            def link(ins):
                n[0] += 1
                ins.then_inc(pool_own, 1)
                pool.wait_ge(pool_own, n[0])

            pool.memset(pads[:, 1, :], 0)
            pool.memset(fpad[:, :], -5.0)
            link(pool.memset(pads[:, 0, :], -1))
            pool.sem_inc(const_ready, 1)
            pool.iota(iota_row[:, :], pattern=[[1, P]], base=0, channel_multiplier=0, allow_small_or_imprecise_dtypes=True)
            pool.iota(iota_col[:, :], pattern=[[0, 1]], base=0, channel_multiplier=1, allow_small_or_imprecise_dtypes=True)
            pool.iota(tile_no[:, :], pattern=[[P, TG]], base=0, channel_multiplier=1, allow_small_or_imprecise_dtypes=True)
            pool.memset(ones[:, :], 1.0)
            pool.memset(node_mask[:, :], 1.0)
            link(pool.memset(ident[:, :], 0.0))
            pool.affine_select(out=ident[:, :], in_=ident[:, :], compare_op=ALU.not_equal, fill=1.0, base=0,
                               pattern=[[-1, P]], channel_multiplier=1)
            link(pool.affine_select(out=node_mask[:, :], in_=node_mask[:, :], compare_op=ALU.is_ge, fill=0.0,
                                    base=N - 1, pattern=[[-P, NB]], channel_multiplier=-1))
            pool.sem_inc(const_ready, 1)

            pool.wait_ge(padded, 16 * (4 + 2 * (E % P > 0)))
            pool.wait_ge(runs_ready, 1)
            for g in range(TG):
                for a, r in ((dst_d, dst_r), (src_d, src_r)):
                    pool.indirect_dma_start(r[:, g * P:(g + 1) * P], None, a[:, :],
                                            bass.IndirectOffsetOnAxis(ap=run_i[:, g:g + 1], axis=0)).then_inc(rows_in, 16)

            def gather(l, c, first):
                x2 = par(c)
                if not first:
                    pool.wait_ge(scored, lin(c, NG, -NG))
                pool.tensor_copy(idx[:, x2, :], src_e[:, bass.ds(local(l, c, CT, 0), CT)]).then_inc(idx_ready, 1)
                pool.wait_ge(idx_ready, lin(c, 1, 1))
                for g in range(NG):
                    at_least(pool, prepared, lin(c, NG, g + 1 - 2 * NG))
                    pool.sem_inc(pool_go, 1)
                    for k in range(GT):
                        t = g * GT + k
                        pool.indirect_dma_start(rows(l, x2, t, 1)[:, 0, :], None, table[l][:, :],
                                                bass.IndirectOffsetOnAxis(ap=idx[:, x2, t:t + 1], axis=0)
                                                ).then_inc(gathered[x2 * NG + g], 16)

            for l in range(NL):
                if l == 0:
                    pool.wait_ge(lists_ready, 1)
                pool.wait_ge(table_out, 16 * (l + 1))
                for c in range(2):
                    gather(l, (None, l * NC + c), l == 0)
                with pool.Fori(0, NC // 2 - 1) as i:
                    for k in (2, 3):
                        gather(l, (i, l * NC + k), False)

        @block.scalar
        def _(act):
            def relu(l, c, g):
                v = lin(c, NG, g)
                act.wait_ge(z_ready, lin(c, NG, g + 1))
                at_least(act, scored, lin(c, NG, g - 1))
                nk = FP[l] // P
                act.activation(relu_z[:, g % 2, :, 0:nk, :],
                               ps_z[:, g % 2, :, :].rearrange("p a b -> p (a b)")[:, 0:GT * nk * P]
                               .rearrange("p (t k e) -> p t k e", t=GT, k=nk), ACT.Relu).then_inc(relu_ready, 1)

            def softmax(l, c):
                act.wait_ge(sm_v, lin(c, SV, 17))
                act.activation(prob_t[:, :], shifted[:, :], ACT.Exp).then_inc(sm_a, 1)
                act.activation(rescale[:, :], carry_col[:, 2:], ACT.Exp).then_inc(sm_a, 1)
                act.wait_ge(sm_p, lin(c, SP_, 4))
                for d, o in ((prob_e, PM_PROB), (max_e, PM_MAX)):
                    act.activation(d[:, par(c), :, :], ps_m[:, o:o + P].rearrange("p (h t) -> p t h", h=HMAX),
                                   ACT.Copy).then_inc(sm_a, 1)

            def row_penalties(l, c):
                at_least(act, sm_v, lin(c, SV, 7 - SV))
                for d, v in ((heads_pen_f[:, :, 1:CT + 1], row_pen_f), (heads_pen_b[:, :, :], row_pen_b)):
                    ins = act.activation(d, v[:, bass.ds(local(l, c, 1, 0), 1), :].broadcast_to([1, HMAX, CT]), ACT.Copy)
                ins.then_inc(row_pen, 1)

            def weight_columns(l, c, g):
                h = HS[l]
                w = weighted[:, g % 2, :, :]
                act.wait_ge(sm_a, lin(c, SA, 4))
                at_least(act, summed, lin(c, CT, GT * (g - 1)))
                t = slice(g * GT, (g + 1) * GT)
                act.activation(w[:, :, 0:h * (F + 1)].rearrange("p t (h f) -> p t h f", h=h)[:, :, :, F],
                               prob_e[:, par(c), t, 0:h], ACT.Copy)
                act.activation(w[:, :, h * (F + 1):h * (F + 2)], max_e[:, par(c), t, 0:h],
                               ACT.Copy).then_inc(columns, 1)

            def run_chunk(l):
                def run(c, scores, soft, plan):
                    for g, _, ahead in plan:
                        if scores:
                            relu(l, c, g)
                        if soft and g == 0:
                            row_penalties(l, shift(c, -1))
                        if soft and g == 3:
                            softmax(l, shift(c, -1))
                        if ahead:
                            weight_columns(l, *ahead)
                return run

            act.wait_ge(lists_ready, 1)
            for l in range(NL):
                for b in range(NB):
                    act.wait_ge(turned, l * NB + b + 1)
                    act.activation(turned_in(l)[0:KP[l], :, b * P:(b + 1) * P],
                                   ps_z[0:KP[l], b % 4 // 2, b % 2, 0:KC[l] * P].rearrange("p (k n) -> p k n", k=KC[l]),
                                   ACT.Copy).then_inc(turned_out, 1)
                edge_phase(act, l, run_chunk(l))
                act.wait_ge(merge_ready, l + 1)
                for k in (2, 3):
                    ins = act.activation(small[:, k, :], small[:, k, :], ACT.Exp)
                ins.then_inc(merge_exp, 1)
            for q, v in enumerate((tiny[:, 3:4], small[:, 2, 0:NB])):
                act.wait_ge(root_go, q + 1)
                act.activation(y_root(q), v, ACT.Sqrt).then_inc(root_done, 1)

        @block.tensor
        def _(pe):
            pe.wait_ge(const_ready, 2)
            pe.wait_ge(counts_ready, 1)
            pe.matmul(ps_m[:, 0:NB - 1], ones[0:EDIV, :], cnt[0:EDIV, :], start=True, stop=True).then_inc(counts_sum, 1)
            pe.wait_ge(keys_ready, 1)
            for g in range(TG):
                if g >= 2:
                    pe.wait_ge(taken, g - 1)
                for k, w in enumerate((loc_w, src_w)):
                    ins = pe.transpose(ps_o[:, g % 2, k * P:(k + 1) * P], w[:, g * P:(g + 1) * P], ident[:, :])
                ins.then_inc(prep_turned, 1)

            def z_group(l, c, g):
                x2, nk = par(c), FP[l] // P
                blks = [block_of(pe, l, c, g * GT + k) for k in range(GT)]
                if g % 2 == 0:
                    pe.wait_ge(oht_ready, lin(c, NG // 2, g // 2 + 1))
                pe.wait_ge(gathered[x2 * NG + g], lin(c, 32, 64 - 32 * x2))
                z = ps_z[:, g % 2, :, :].rearrange("p a b -> p (a b)")
                for k in range(GT):
                    t = g * GT + k
                    for q in range(nk):
                        zk = z[:, (k * nk + q) * P:(k * nk + q + 1) * P]
                        pe.matmul(zk, rows(l, x2, t, 1)[:, 0, q * P:(q + 1) * P], ident[:, :],
                                  is_transpose=True, start=True, stop=False)
                        for r in range(PARTS):
                            ins = pe.matmul(zk, xr_parts[:, r, bass.ds(blks[k], 1), q * P:(q + 1) * P].rearrange("p b f -> p (b f)"),
                                            oht[:, g // 2 % 2, (g % 2 * GT + k) * P:(g % 2 * GT + k + 1) * P],
                                            start=False, stop=(r == PARTS - 1))
                ins.then_inc(z_ready, 1)

            def score_group(l, c, g):
                h, nk = HS[l], FP[l] // P
                pe.wait_ge(relu_ready, lin(c, NG, g + 1))
                for k in range(GT):
                    s = ps_s[:, par(c), g * GT + k:g * GT + k + (h - 1) * CT + 1:CT]
                    for q in range(nk):
                        ins = pe.matmul(s, relu_z[:, g % 2, k, q, :], att_bd[:, q, 0:h], start=(q == 0), stop=(q == nk - 1))
                ins.then_inc(scored, 1)

            def softmax(l, c, step):
                pe.wait_ge(sm_v, lin(c, SV, (1, 3, 12, 18)[step]))
                if step == 0:
                    at_least(pe, sm_a, lin(c, SA, 0))
                    ins = pe.transpose(ps_m[:, PM_T:PM_T + P], score[:, :], ident[:, :])
                elif step == 1:
                    pe.transpose(ps_m[0:1, PM_L:PM_L + P], run_fwd[:, P - 1:P], ident[:, :])
                    ins = pe.transpose(ps_m[0:1, PM_F:PM_F + P], run_bwd[:, 0:1], ident[:, :])
                elif step == 2:
                    for q, v in enumerate((carry_f, carry_b)):
                        pe.matmul(ps_m[:, PM_C + q:PM_C + q + 1], v[:, :, :].rearrange("o h t -> o (h t)"),
                                  ones[0:1, 0:1], start=True, stop=True)
                    ins = pe.matmul(ps_m[:, PM_B:PM_B + HMAX], first_hot[:, :], boundary[:, 1, :], start=True, stop=True)
                else:
                    pe.wait_ge(sm_a, lin(c, SA, 1))
                    pe.transpose(ps_m[:, PM_PROB:PM_PROB + P], prob_t[:, :], ident[:, :])
                    ins = pe.transpose(ps_m[:, PM_MAX:PM_MAX + P], max_last[:, :], ident[:, :])
                ins.then_inc(sm_p, 1)

            def sum_group(l, c, g):
                pe.wait_ge(prepared, lin(c, NG, g + 1))
                pe.wait_ge(columns, lin(c, NG, g + 1))
                for k in range(GT):
                    at_least(pe, flushed, lin(c, CT, g * GT + k - 1))
                    pe.matmul(ps_o[:, k % 2, 0:WS[l]], oh[:, g % 2, k, :], weighted[:, g % 2, k, 0:WS[l]],
                              start=True, stop=True).then_inc(summed, 1)

            def run_chunk(l):
                def run(c, scores, soft, plan):
                    for g, sums, _ in plan:
                        if g == 0 and soft:
                            score_group(l, shift(c, -1), NG - 1)
                        if g > 0 and scores:
                            score_group(l, c, g - 1)
                        if scores:
                            z_group(l, c, g)
                        if soft and g < SP_:
                            softmax(l, shift(c, -1), g)
                        if sums:
                            sum_group(l, *sums)
                return run

            def total(q):
                pe.wait_ge(stat_ready, q + 1)
                pe.matmul(ps_m[:, q:q + 1], ones[:, :], tiny[:, q:q + 1], start=True, stop=True).then_inc(stat_sum, 1)

            for l in range(NL):
                pe.wait_ge(h_ready, l + 1)
                if l == 0:
                    pe.wait_ge(x_in, 32)
                h = x_place if l == 0 else area(0, KI[l])
                for b in range(NB):
                    at_least(pe, turned_out, l * NB + b - 3 if b >= 4 else 0)
                    for k in range(KC[l]):
                        ins = pe.transpose(ps_z[0:KP[l], b % 4 // 2, b % 2, k * P:(k + 1) * P],
                                           h[:, b, k * P:k * P + KP[l]], ident[:, :])
                    ins.then_inc(turned, 1)
                pe.wait_ge(weights_in, W_DMAS[l])
                pe.wait_ge(turned_out, (l + 1) * NB)
                for b in range(NB):
                    at_least(pe, taken, TG + l * NB + b - 1 if b >= 2 else TG)
                    for k in range(KC[l]):
                        ins = pe.matmul(ps_o[:, b % 2, 0:2 * FS[l]], turned_in(l)[0:KP[l], k, b * P:(b + 1) * P],
                                        weights[0:KP[l], k, 0:2 * FS[l]], start=(k == 0), stop=(k == KC[l] - 1))
                    ins.then_inc(projected, 1)
                pe.wait_ge(att_ready, l + 1)
                edge_phase(pe, l, run_chunk(l))
            total(0)
            total(1)

        @block.vector
        def _(dve):
            n = [0]

            def link(ins):
                n[0] += 1
                ins.then_inc(dve_own, 1)
                dve.wait_ge(dve_own, n[0])

            dve.memset(acc[:, :, :], 0.0)
            dve.memset(run_row[:, :, :], -BIG)
            dve.memset(score[:, :], 0.0)
            dve.memset(heads_pen_f[:, :, :], -BIG)
            dve.memset(row_pen_b[:, :, :], -BIG)
            dve.memset(carry_pen_b[:, :, :], -BIG)
            dve.memset(czero, 0.0)
            link(dve.memset(carry_b[:, :, :], -BIG))
            dve.sem_inc(x_room, 1)
            dve.sem_inc(h_ready, 1)

            dve.wait_ge(dst_in, 16)
            link(dve.tensor_copy(dst_f[0:EDIV, :], dst_l[0:EDIV, :]))
            for b in range(1, NB):
                link(dve.tensor_scalar(junk[0:EDIV, :], dst_f[0:EDIV, :], float(b * P), None, ALU.is_lt))
                link(dve.tensor_reduce(cnt[0:EDIV, b - 1:b], junk[0:EDIV, :], AX.X, ALU.add))
            dve.sem_inc(counts_ready, 1)
            dve.wait_ge(counts_sum, 1)
            link(dve.tensor_copy(cnt_all, ps_m[:, 0:NB - 1]))
            link(dve.tensor_copy(cint, cnt_all))
            link(dve.tensor_scalar(cint, cint, P.bit_length() - 1, None, ALU.arith_shift_right))
            link(dve.tensor_copy(cfloor, cint))
            link(dve.tensor_scalar(cmod, cfloor, float(P), None, ALU.mult))
            link(dve.tensor_tensor(cdelta, cnt_all, cmod, ALU.is_gt))
            link(dve.tensor_tensor_scan(cmod, cdelta, czero, 0.0, ALU.add, ALU.add))
            link(dve.tensor_tensor(cfloor, cfloor, cmod, ALU.add))
            dve.wait_ge(const_ready, 2)
            ge3 = ge.rearrange("p (g b) -> p g b", g=TG)
            ged3 = ged.rearrange("p (g b) -> p g b", g=TG)

            def wide(v):
                return v.unsqueeze(1).broadcast_to([P, TG, NB - 1])

            link(dve.tensor_tensor(ge3, tile_no[:, :].unsqueeze(2).broadcast_to([P, TG, NB - 1]), wide(cfloor), ALU.is_ge))
            link(dve.tensor_tensor(ged3, ge3, wide(cdelta), ALU.mult))
            link(dve.tensor_reduce(blk_f, ge3, AX.X, ALU.add))
            link(dve.tensor_reduce(run_f, ged3, AX.X, ALU.add))
            link(dve.tensor_tensor(run_f, tile_no[:, :], run_f, ALU.subtract))
            link(dve.tensor_scalar(run_i, run_f, float(OT), None, ALU.min))
            dve.sem_inc(runs_ready, 1)
            link(dve.tensor_copy(blk_i, blk_f))
            link(dve.tensor_scalar(blk128, blk_f, float(P), None, ALU.mult))
            dve.wait_ge(rows_in, 16 * 2 * TG)
            dst3, loc3 = (v.rearrange("p (g e) -> p g e", g=TG) for v in (dst_r, loc_w))
            link(dve.tensor_tensor(loc3, dst3, blk128.unsqueeze(2).broadcast_to([P, TG, P]), ALU.subtract))
            link(dve.tensor_scalar(valid, loc_w, 0.0, None, ALU.is_ge))
            link(dve.tensor_scalar(key_w, loc_w, float(P), None, ALU.is_lt))
            link(dve.tensor_tensor(valid, valid, key_w, ALU.mult))
            link(dve.tensor_scalar(key_w, dst_r, 1.0, None, ALU.add))
            link(dve.tensor_tensor(key_w, key_w, valid, ALU.mult))
            link(dve.tensor_scalar(loc_w, loc_w, 1.0, None, ALU.add))
            link(dve.tensor_tensor(loc_w, loc_w, valid, ALU.mult))
            link(dve.tensor_scalar(loc_w, loc_w, -1.0, None, ALU.add))
            link(dve.tensor_copy(loc_bf, loc_w))
            link(dve.tensor_copy(src_w, src_r))
            dve.sem_inc(keys_ready, 1)
            for g in range(TG):
                dve.wait_ge(prep_turned, g + 1)
                dve.tensor_copy(loc_e[:, g * P:(g + 1) * P], ps_o[:, g % 2, 0:P])
                link(dve.tensor_copy(src_e[:, g * P:(g + 1) * P], ps_o[:, g % 2, P:2 * P]))
                dve.sem_inc(taken, 1)
            dve.sem_inc(prep_taken, 1)
            dve.wait_ge(keys_in, 16 * (1 + 3 * HMAX + 2))
            link(dve.tensor_tensor(key_t[1], key_t[0], key_t[1], ALU.not_equal))
            link(dve.tensor_scalar(pen_f[:, :, :], key_t[1], -BIG, None, ALU.mult))
            link(dve.tensor_tensor(key_t[2], key_t[0], key_t[2], ALU.not_equal))
            link(dve.tensor_scalar(pen_b[:, :, ::-1], key_t[2], -BIG, None, ALU.mult))
            link(dve.tensor_tensor(cont, first_key, last_key, ALU.is_equal))
            link(dve.tensor_tensor(joined, first_key[:, 0:NT], last_key[:, 1:NT + 1], ALU.is_equal))

            def penalty(o, v):
                link(dve.tensor_scalar(o, v, -1.0, BIG, ALU.add, ALU.mult))

            cont_before = cont[:, 0:NT].rearrange("o (c t) -> o c t", t=CT)
            cont_after = cont[:, 1:NT + 1].rearrange("o (c t) -> o c t", t=CT)
            penalty(carry_pen_f[:, :, :], cont_before)
            penalty(carry_pen_b[:, :, 0:CT - 1], cont_after[:, :, 0:CT - 1])
            joined3 = joined.rearrange("o (c t) -> o c t", t=CT)
            both = first_key[:, 0:NT].rearrange("o (c t) -> o c t", t=CT)
            link(dve.tensor_tensor(both, joined3, cont_before, ALU.mult))
            penalty(row_pen_f[:, :, :], both)
            link(dve.tensor_tensor(both, joined3, cont_after, ALU.mult))
            penalty(row_pen_b[:, :, 0:CT - 1], both[:, :, 0:CT - 1])
            link(dve.tensor_copy(chunk_cont[:, :], cont_before[:, :, 0]))
            dve.sem_inc(lists_ready, 1)

            def node_phase(l):
                hh, fs = HS[l], FS[l]
                dve.wait_ge(weights_in, W_DMAS[l])
                link(dve.tensor_scalar(att_lo[:, 0:fs], att_hi[:, 0:fs], SLOPE_ATT, None, ALU.mult))
                link(dve.tensor_scalar(att_hi[:, 0:fs], att_hi[:, 0:fs], 1.0 - SLOPE_ATT, None, ALU.mult))
                link(dve.tensor_scalar(att_bd[:, :, :], att_bd[:, :, :], 1.0 - SLOPE_ATT, None, ALU.mult))
                dve.sem_inc(att_ready, 1)
                dve.wait_ge(turned, (l + 1) * NB)
                dve.memset(acc[:, :, :], 0.0)
                tab = area(0, WR[l])
                if FP[l] > fs:
                    dve.memset(tab[:, :, fs:FP[l]], 0.0)
                    dve.memset(xr_parts[:, :, :, fs:FP[l]], 0.0)
                xr, z, q, rest = (tmp[:, k, 0:fs] for k in range(4))

                def heads(v):
                    return v.rearrange("p (h f) -> p h f", h=hh)

                for b in range(NB):
                    xl, pl = tab[:, b, 0:fs], tab[:, b, FP[l]:FP[l] + hh]
                    part = [xr_parts[:, r, b, 0:fs] for r in range(PARTS)]
                    dve.wait_ge(projected, l * NB + b + 1)
                    dve.tensor_tensor(xl, ps_o[:, b % 2, 0:fs], bias_in[:, 0:fs], ALU.add)
                    link(dve.tensor_tensor(xr, ps_o[:, b % 2, fs:2 * fs], bias_in[:, fs:2 * fs], ALU.add))
                    dve.sem_inc(taken, 1)
                    dve.tensor_tensor(z, xl, xr, ALU.add)
                    dve.tensor_tensor(q, xl, att_lo[:, 0:fs], ALU.mult)
                    link(dve.tensor_copy(part[0], xr))
                    dve.scalar_tensor_tensor(out=z, in0=z, scalar=0.0, in1=att_hi[:, 0:fs], op0=ALU.max, op1=ALU.mult)
                    dve.tensor_reduce(pl, heads(q), AX.X, ALU.add)
                    link(dve.tensor_tensor(rest, xr, part[0], ALU.subtract))
                    dve.tensor_reduce(s_self[:, b, 0:hh], heads(z), AX.X, ALU.add)
                    link(dve.tensor_copy(part[1], rest))
                    dve.tensor_tensor(part[2], rest, part[1], ALU.subtract)
                    link(dve.tensor_tensor(s_self[:, b, 0:hh], s_self[:, b, 0:hh], pl, ALU.add))
                dve.sem_inc(table_ready, 1)

            def one_hot_t(l, c, j):
                dve.wait_ge(loc_in[j % 2], lin(c, 32, 16 * (j // 2 + 1)))
                at_least(dve, z_ready, lin(c, NG, 2 * j - 2))
                dve.tensor_scalar(oht[:, j % 2, :], locbc[:, j % 2, :], iota_col[:, 0:1], None,
                                  ALU.is_equal).then_inc(oht_ready, 1)

            def softmax(l, c, step):
                def done(k):
                    dve.wait_ge(sm_v, lin(c, SV, k))

                hh = HS[l]
                cl = local(l, c, 1, 0)

                def of_chunk(v):
                    return v[:, bass.ds(cl, 1)]

                def flat(v):
                    return v.rearrange("p c e -> p (c e)")

                turned_score = ps_m[:, PM_T:PM_T + P]
                if step == 0:
                    dve.wait_ge(scored, lin(c, NG, NG))
                    dve.tensor_tensor(score[:, 0:hh * CT].rearrange("p (h t) -> p h t", h=hh),
                                      ps_s[:, par(c), 0:hh * CT].rearrange("p (h t) -> p h t", h=hh),
                                      rows(l, par(c), 0, CT)[:, :, FP[l]:FP[l] + hh].rearrange("p t h -> p h t"),
                                      ALU.add).then_inc(sm_v, 1)
                elif step == 1:
                    dve.wait_ge(sm_p, lin(c, SP_, 1))
                    dve.tensor_tensor_scan(run_fwd[:, :], flat(of_chunk(pen_f)), turned_score, -BIG,
                                           ALU.add, ALU.max).then_inc(sm_v, 1)
                    dve.tensor_tensor_scan(run_bwd[:, ::-1], flat(of_chunk(pen_b)), turned_score[:, ::-1],
                                           -BIG, ALU.add, ALU.max).then_inc(sm_v, 1)
                elif step == 2:
                    dve.wait_ge(sm_p, lin(c, SP_, 2))
                    dve.tensor_copy(run_in[:, :, 1:CT + 1], ps_m[0:1, PM_L:PM_L + P].rearrange("o (h t) -> o h t", h=HMAX)
                                    ).then_inc(sm_v, 1)
                    dve.tensor_copy(run_in[:, :, 0:1], run_row[:, :, CT:CT + 1]).then_inc(sm_v, 1)
                    done(5)
                    dve.wait_ge(row_pen, lin(c, 1, 1))
                    dve.tensor_tensor_scan(run_row[:, :, :].rearrange("o h t -> o (h t)"),
                                           heads_pen_f[:, :, :].rearrange("o h t -> o (h t)"),
                                           run_in[:, :, :].rearrange("o h t -> o (h t)"), -BIG,
                                           ALU.add, ALU.max).then_inc(sm_v, 1)
                    dve.tensor_tensor_scan(back_row[:, :, :].rearrange("o h t -> o (h t)")[:, ::-1],
                                           heads_pen_b[:, :, :].rearrange("o h t -> o (h t)")[:, ::-1],
                                           ps_m[0:1, PM_F:PM_F + P][:, ::-1], -BIG,
                                           ALU.add, ALU.max).then_inc(sm_v, 1)
                    done(6)
                    dve.tensor_tensor(carry_f[:, :, :], run_row[:, :, 0:CT],
                                      of_chunk(carry_pen_f).broadcast_to([1, HMAX, CT]), ALU.add).then_inc(sm_v, 1)
                    done(7)
                    dve.tensor_tensor(carry_b[:, :, 0:CT - 1], back_row[:, :, 1:CT],
                                      of_chunk(carry_pen_b)[:, :, 0:CT - 1].broadcast_to([1, HMAX, CT - 1]),
                                      ALU.add).then_inc(sm_v, 1)
                    dve.tensor_tensor(boundary[:, 0, :], run_in[:, :, 0], back_row[:, :, 0],
                                      ALU.subtract).then_inc(sm_v, 1)
                    done(10)
                    dve.tensor_scalar(boundary[:, 1, :], boundary[:, 0, :], 0.0, chunk_cont[:, bass.ds(cl, 1)],
                                      ALU.min, ALU.mult).then_inc(sm_v, 1)
                    dve.tensor_scalar(first_hot[:, :], iota_row[0:1, :], loc_e[0:1, bass.ds(local(l, c, CT, 0), 1)], None,
                                      ALU.is_equal).then_inc(sm_v, 1)
                else:
                    dve.wait_ge(sm_p, lin(c, SP_, 3))
                    dve.tensor_copy(carry_col[:, :], ps_m[:, PM_C:PM_B + HMAX]).then_inc(sm_v, 1)
                    done(13)
                    dve.tensor_tensor_scan(run_fwd[:, :], flat(of_chunk(pen_f)), turned_score, carry_col[:, 0:1],
                                           ALU.add, ALU.max).then_inc(sm_v, 1)
                    dve.tensor_tensor_scan(run_bwd[:, ::-1], flat(of_chunk(pen_b)), turned_score[:, ::-1],
                                           carry_col[:, 1:2], ALU.add, ALU.max).then_inc(sm_v, 1)
                    done(15)
                    dve.tensor_tensor(edge_max[:, :], run_fwd[:, :], run_bwd[:, :], ALU.max).then_inc(sm_v, 1)
                    done(16)
                    dve.tensor_tensor(shifted[:, :], turned_score, edge_max[:, :], ALU.subtract).then_inc(sm_v, 1)
                    dve.scalar_tensor_tensor(out=max_last[:, ::-1], in0=flat(of_chunk(pen_b)), scalar=-1.0 / BIG,
                                             in1=edge_max[:, ::-1], op0=ALU.mult, op1=ALU.mult).then_inc(sm_v, 1)

            def prepare(l, c, g):
                hh = HS[l]
                dve.wait_ge(sm_a, lin(c, SA, 3))
                for k in range(GT):
                    dve.tensor_scalar(oh[:, g % 2, k, :], iota_row[:, :],
                                      loc_e[:, bass.ds(local(l, c, CT, g * GT + k), 1)], None, ALU.is_equal)
                dve.tensor_tensor(weighted[:, g % 2, :, 0:hh * (F + 1)].rearrange("p t (h f) -> p t h f", h=hh)[:, :, :, 0:F],
                                  rows(l, par(c), g * GT, GT)[:, :, 0:FS[l]].rearrange("p t (h f) -> p t h f", h=hh),
                                  prob_e[:, par(c), g * GT:(g + 1) * GT, 0:hh].unsqueeze(3).broadcast_to([P, GT, hh, F]),
                                  ALU.mult).then_inc(prepared, 1)

            def flush(l, c, g):
                hh = HS[l]

                sums_of = [acc[:, bass.ds(block_of(dve, l, c, g * GT + k), 1), :] for k in range(GT)]
                if g == 0:
                    a = sums_of[0][:, :, 0:hh * (F + 1)].rearrange("p b (h f) -> p (b h) f", h=hh)
                    at_least(dve, flushed, lin(c, CT, 0))
                    dve.tensor_tensor(a, a, rescale[:, 0:hh].unsqueeze(2).broadcast_to([P, hh, F + 1]),
                                      ALU.mult).then_inc(rescaled, 1)
                    dve.wait_ge(rescaled, lin(c, 1, 1))
                for k in range(GT):
                    a = sums_of[k][:, :, 0:WS[l]].rearrange("p b f -> p (b f)")
                    dve.wait_ge(summed, lin(c, CT, g * GT + k + 1))
                    at_least(dve, flushed, lin(c, CT, g * GT + k))
                    dve.tensor_tensor(a, a, ps_o[:, k % 2, 0:WS[l]], ALU.add).then_inc(flushed, 1)

            def run_chunk(l):
                def run(c, scores, soft, plan):
                    for g, sums, ahead in plan:
                        if scores and g == 0:
                            one_hot_t(l, c, 0)
                        if soft and g < 4:
                            softmax(l, shift(c, -1), g)
                        if scores and g % 2 == 1 and g < NG - 1:
                            one_hot_t(l, c, g // 2 + 1)
                        if ahead:
                            prepare(l, *ahead)
                        if sums:
                            flush(l, *sums)
                return run

            def merge(l):
                hh, fs = HS[l], FS[l]
                sums = acc[:, :, 0:hh * (F + 1)].rearrange("p b (h f) -> p b h f", h=hh)
                dve.wait_ge(flushed, (l + 1) * NT)

                def v(k):
                    return small[:, k, :].rearrange("p (b h) -> p b h", b=NB)[:, :, 0:hh]

                l_acc, m_acc, self_ = sums[:, :, :, F], acc[:, :, hh * (F + 1):hh * (F + 2)], s_self[:, :, 0:hh]
                if l == 0 or hh < HMAX:
                    dve.memset(small[:, 2, :], 0.0)
                    link(dve.memset(small[:, 3, :], 0.0))
                link(dve.tensor_scalar(v(0), l_acc, 0.5, -BIG, ALU.is_lt, ALU.mult))
                link(dve.tensor_tensor(v(0), v(0), m_acc, ALU.add))
                link(dve.tensor_tensor(v(1), v(0), self_, ALU.max))
                dve.tensor_tensor(v(2), v(0), v(1), ALU.subtract)
                link(dve.tensor_tensor(v(3), self_, v(1), ALU.subtract))
                dve.sem_inc(merge_ready, 1)
                dve.wait_ge(merge_exp, l + 1)
                link(dve.tensor_tensor(v(4), l_acc, v(2), ALU.mult))
                link(dve.tensor_tensor(v(4), v(4), v(3), ALU.add))
                link(dve.reciprocal(v(5), v(4)))
                dve.tensor_tensor(v(6), v(2), v(5), ALU.mult)
                link(dve.tensor_tensor(v(7), v(3), v(5), ALU.mult))
                x_sums = sums[:, :, :, 0:F]
                dve.tensor_tensor(x_sums, x_sums, v(6).unsqueeze(3).broadcast_to([P, NB, hh, F]), ALU.mult)
                dve.wait_ge(table_again, 16 * (l + 1))
                xs = area(1, WR[l])[:, :, 0:fs].rearrange("p b (h f) -> p b h f", h=hh)
                link(dve.tensor_tensor(xs, xs, v(7).unsqueeze(3).broadcast_to([P, NB, hh, F]), ALU.mult))
                h = area(0, fs)
                link(dve.tensor_tensor(h.rearrange("p b (h f) -> p b h f", h=hh), x_sums, xs, ALU.add))
                link(dve.tensor_tensor(h, h, bias_out[:, 0:fs].unsqueeze(1).broadcast_to([P, NB, fs]), ALU.add))
                link(dve.scalar_tensor_tensor(out=h, in0=h, scalar=SLOPE_OUT, in1=h, op0=ALU.mult, op1=ALU.max))

            for l in range(NL):
                link(dve.memset(att_bd[:, :, :], 0.0))
                dve.sem_inc(att_room, 1)
                node_phase(l)
                edge_phase(dve, l, run_chunk(l))
                merge(l)
                if l < NL - 1:
                    dve.sem_inc(h_ready, 1)

            link(dve.memset(x_place[:, NB - 1:NB, :], 0.0))
            dve.sem_inc(x_again_room, 1)
            dve.wait_ge(x_in, 16 * 6)
            h, sq = area(0, F), area(1, F)

            def over_nodes(v):
                return v.unsqueeze(1).broadcast_to([P, NB, F])

            def over_features(v):
                return v.unsqueeze(2).broadcast_to([P, NB, F])

            def total(q, v):
                link(dve.tensor_reduce(small[:, 0, 0:NB], v, AX.X, ALU.add))
                link(dve.tensor_tensor(small[:, 0, 0:NB], small[:, 0, 0:NB], node_mask[:, :], ALU.mult))
                link(dve.tensor_reduce(tiny[:, q:q + 1], small[:, 0, 0:NB], AX.X, ALU.add))
                dve.sem_inc(stat_ready, 1)
                dve.wait_ge(stat_sum, q + 1)
                link(dve.tensor_scalar(tiny[:, 2 + q:3 + q], ps_m[:, q:q + 1], 1.0 / (N * F), None, ALU.mult))

            def inverse_root(y, v, t, q):
                dve.sem_inc(root_go, 1)
                dve.wait_ge(root_done, q + 1)
                link(dve.reciprocal(y, y_root(q)))
                link(dve.tensor_tensor(t, y, y, ALU.mult))
                link(dve.tensor_tensor(t, t, v, ALU.mult))
                link(dve.tensor_scalar(t, t, -0.5, 1.5, ALU.mult, ALU.add))
                link(dve.tensor_tensor(y, y, t, ALU.mult))

            link(dve.tensor_tensor(h, h, x_place, ALU.add))
            total(0, h)
            link(dve.tensor_scalar(h, h, tiny[:, 2:3], None, ALU.subtract))
            link(dve.tensor_tensor(sq, h, h, ALU.mult))
            total(1, sq)
            link(dve.tensor_scalar(tiny[:, 3:4], tiny[:, 3:4], EPS, None, ALU.add))
            inverse_root(tiny[:, 4:5], tiny[:, 3:4], tiny[:, 5:6], 0)
            link(dve.tensor_scalar(h, h, tiny[:, 4:5], None, ALU.mult))
            link(dve.tensor_tensor(h, h, over_nodes(lnw[:, 0, :]), ALU.mult))
            link(dve.tensor_tensor(h, h, over_nodes(lnw[:, 1, :]), ALU.add))
            link(dve.tensor_tensor(h, h, x_place, ALU.add))
            mean, rstd, var = (small[:, k, 0:NB] for k in range(3))
            link(dve.tensor_reduce(mean, h, AX.X, ALU.add))
            link(dve.tensor_scalar(mean, mean, 1.0 / F, None, ALU.mult))
            link(dve.tensor_tensor(h, h, over_features(mean), ALU.subtract))
            link(dve.tensor_tensor(sq, h, h, ALU.mult))
            link(dve.tensor_reduce(rstd, sq, AX.X, ALU.add))
            link(dve.tensor_scalar(var, rstd, 1.0 / F, EPS, ALU.mult, ALU.add))
            inverse_root(rstd, var, small[:, 3, 0:NB], 1)
            link(dve.tensor_tensor(h, h, over_features(rstd), ALU.mult))
            dve.sem_inc(result_ready, 1)


LAYERS = 4
PART_NAMES = ["Wl", "bl", "Wr", "br", "att", "bias"]


def kernel(**inputs):
    import numpy as np
    import concourse.bacc as bacc
    from concourse import mybir as mb
    from concourse.bass_utils import run_bass_kernel_spmd

    nc = bacc.Bacc("TRN2", target_bir_lowering=False, num_devices=1)
    arrays = {}

    def given(name):
        a = np.ascontiguousarray(inputs[name])
        arrays[f"in_{name}"] = a
        return nc.dram_tensor(f"in_{name}", a.shape, mb.dt.from_np(a.dtype), kind="ExternalInput").ap()

    x, src, dst = (given(n) for n in ("x", "src", "dst"))
    layers = [{n: given(f"L0_gnn_l{l}_{n}") for n in PART_NAMES} for l in range(LAYERS)]
    ln_w, ln_b = given("L0_gnn_ln_w"), given("L0_gnn_ln_b")
    out = nc.dram_tensor("out", x.shape, mb.dt.float32, kind="ExternalOutput").ap()
    program(nc, x, src, dst, layers, ln_w, ln_b, out)
    r = run_bass_kernel_spmd(nc, [arrays], core_ids=[0])
    return r.results[0]["out"]
```

```python
from contextlib import ExitStack

import concourse.bass as bass
from concourse import mybir

F32 = mybir.dt.float32
BF16 = mybir.dt.bfloat16
I32 = mybir.dt.int32
ALU = mybir.AluOpType
ACT = mybir.ActivationFunctionType
AX = mybir.AxisListType

P = 128
CT = 32
GT = 4
NG = CT // GT
HMAX = 4
LAG = NG + 6
BIG = 2.0 ** 100
SLOPE_ATT = 0.2
SLOPE_OUT = 0.01
EPS = 1e-5
PARTS = 3

MG = 7
SV = 18
SP_ = 4
SA = 4


def ceil_div(a, b):
    return -(-a // b)


def lin(c, a, b):
    i, k = c
    return a * k + b if i is None else i * (2 * a) + (a * k + b)


def shift(c, d):
    return (c[0], c[1] + d)


def program(nc, x, src, dst, layers, ln_w, ln_b, out):
    N, F = x.shape
    E = src.shape[0]
    NB = ceil_div(N, P)
    OT = ceil_div(E, P)
    NC = ceil_div(OT + NB - 1, CT)
    NC += NC % 2
    NT = NC * CT
    TG = ceil_div(NT, P)
    NL = len(layers)
    HS = [lay["att"].shape[0] for lay in layers]
    FS = [h * F for h in HS]
    FP = [max(f, P) for f in FS]
    WR = [FP[l] + HS[l] for l in range(NL)]
    WS = [FS[l] + 2 * HS[l] for l in range(NL)]
    KI = [F] + FS[:-1]
    KC = [ceil_div(k, P) for k in KI]
    KP = [min(k, P) for k in KI]
    WROW, WSUM, FMAX = max(WR), max(WS), max(FS)
    AREA = NB * WROW
    EDIV = max(d for d in range(1, P + 1) if E % d == 0)
    EROW = E // EDIV
    LASTN = N - (NB - 1) * P
    NPAD = (OT + 1) * P - E
    W_DMAS = [0]
    for l in range(NL):
        W_DMAS.append(W_DMAS[-1] + 16 * (2 * KC[l] + HS[l]))
    W_DMAS = W_DMAS[1:]
    V_DMAS = 16 * 3
    STARTS = [NB * q // MG for q in range(MG + 1)]
    group_of = [q for q in range(MG) for _ in range(STARTS[q], STARTS[q + 1])]

    with ExitStack() as ctx:
        def sb(name, shape, dt=F32):
            return ctx.enter_context(nc.sbuf_tensor(name, shape, dt))

        def sem(name):
            return ctx.enter_context(nc.semaphore(name))

        def dram(name, shape, dt=F32):
            return nc.dram_tensor(name, shape, dt, kind="Internal").ap()

        dst_d = dram("dst_padded", (OT + 1, P), I32)
        src_d = dram("src_padded", (OT + 1, P), I32)
        loc_d = dram("loc_rows", (NT + 2 * GT, P), BF16)
        key_d = dram("key_rows", ((TG * P + 2) * P,))
        blk_d = dram("block_of_tile", (TG * P,), I32)
        table = [dram(f"table{l}", (NB * P, WR[l])) for l in range(NL)]

        ring = sb("ring", [P, 2 * CT * WROW])
        acc = sb("acc", [P, NB, WSUM])
        xr_parts = sb("xr_parts", [P, PARTS, NB, FMAX], BF16)
        s_self = sb("s_self", [P, NB, HMAX])
        ident = sb("ident", [P, P])
        iota_row = sb("iota_row", [P, P])
        iota_col = sb("iota_col", [P, 1])
        tile_no = sb("tile_no", [P, TG])
        block_edge = sb("block_edge", [P, NB - 1])
        ones = sb("ones", [P, P])
        pads = sb("pads", [1, 2, NPAD], I32)
        fpad = sb("fpad", [1, P])
        loc_e = sb("loc_e", [P, TG * P])
        src_e = sb("src_e", [P, TG * P], I32)
        block_row = sb("block_row", [1, NT + 1], I32)
        pen_f = sb("pen_f", [P, NC, P], BF16)
        pen_b = sb("pen_b", [P, NC, P], BF16)
        chunk_cont = sb("chunk_cont", [1, NC])
        row_pen_f = sb("row_pen_f", [1, NC, CT], BF16)
        row_pen_b = sb("row_pen_b", [1, NC, CT], BF16)
        heads_pen_f = sb("heads_pen_f", [1, HMAX, CT + 1])
        heads_pen_b = sb("heads_pen_b", [1, HMAX, CT])
        carry_pen_f = sb("carry_pen_f", [1, NC, CT], BF16)
        carry_pen_b = sb("carry_pen_b", [1, NC, CT], BF16)
        idx = sb("idx", [P, 2, CT], I32)
        locbc = sb("locbc", [P, 2, 2 * GT * P], BF16)
        oht = sb("oht", [P, 2, 2 * GT * P], BF16)
        oh = sb("oh", [P, 2, GT, P])
        relu_z = sb("relu_z", [P, 2, GT, 2, P])
        weighted = sb("weighted", [P, 2, GT, WSUM])
        score = sb("score", [P, P])
        run_fwd = sb("run_fwd", [P, P])
        run_bwd = sb("run_bwd", [P, P])
        edge_max = sb("edge_max", [P, P])
        shifted = sb("shifted", [P, P])
        max_last = sb("max_last", [P, P])
        prob_t = sb("prob_t", [P, P])
        prob_e = sb("prob_e", [P, 2, CT, HMAX])
        max_e = sb("max_e", [P, 2, CT, HMAX])
        run_in = sb("run_in", [1, HMAX, CT + 1])
        run_row = sb("run_row", [1, HMAX, CT + 1])
        back_row = sb("back_row", [1, HMAX, CT])
        carry_f = sb("carry_f", [1, HMAX, CT])
        carry_b = sb("carry_b", [1, HMAX, CT])
        boundary = sb("boundary", [1, 2, HMAX])
        first_hot = sb("first_hot", [1, P])
        carry_col = sb("carry_col", [P, 2 + HMAX])
        rescale = sb("rescale", [P, HMAX])
        bias_out = sb("bias_out", [P, FMAX])
        att_hi = sb("att_hi", [P, FMAX])
        att_lo = sb("att_lo", [P, FMAX])
        att_bd = sb("att_bd", [P, 2, HMAX])
        node_mask = sb("node_mask", [P, NB])
        bias_part = sb("bias_part", [PARTS, 2, 2 * FMAX], BF16)
        bias_rows = sb("bias_rows", [PARTS, 2 * FMAX], BF16)
        ones_rows = sb("ones_rows", [PARTS, P], BF16)
        lnw = sb("lnw", [P, 2, F])
        tiny = sb("tiny", [P, 8])

        ps_z = ctx.enter_context(nc.psum_tensor("ps_z", [P, 2, 2, 512], F32))
        ps_s = ctx.enter_context(nc.psum_tensor("ps_s", [P, 2, 256], F32))
        ps_m = ctx.enter_context(nc.psum_tensor("ps_m", [P, 512], F32))
        ps_o = ctx.enter_context(nc.psum_tensor("ps_o", [P, 2, 512], F32))
        assert 2 * AREA + 4 * FMAX + 8 * NB * HMAX <= 2 * CT * WROW
        spare = ring[:, 2 * AREA:]
        weights = spare[:, 0:4 * FMAX].rearrange("p (k f) -> p k f", k=2)
        small = spare[:, 4 * FMAX:4 * FMAX + 8 * NB * HMAX].rearrange("p (k n) -> p k n", k=8)
        tmp = relu_z[:, :, :, :, :].rearrange("p a t k e -> p (a t k e)").rearrange("p (k f) -> p k f", f=FMAX)

        assert AREA + 4 * FMAX <= CT * WR[0] and max(WR) == WR[0] and (NC - 1) % 2 == 1
        bias_in, bias_rest = (ring[0:PARTS, AREA + k * 2 * FMAX:AREA + (k + 1) * 2 * FMAX] for k in range(2))

        PM_T, PM_L, PM_F, PM_C, PM_B = 0, P, 2 * P, 3 * P, 3 * P + 2
        PM_PROB, PM_MAX = PM_L, PM_F

        dst_in = sem("dst_in")
        padded = sem("padded")
        const_ready = sem("const_ready")
        pool_own = sem("pool_own")
        dve_own = sem("dve_own")
        counts_ready = sem("counts_ready")
        counts_sum = sem("counts_sum")
        runs_ready = sem("runs_ready")
        rows_in = sem("rows_in")
        keys_ready = sem("keys_ready")
        prep_turned = sem("prep_turned")
        prep_taken = sem("prep_taken")
        stored = sem("stored")
        keys_in = sem("keys_in")
        lists_ready = sem("lists_ready")
        x_room = sem("x_room")
        x_in = sem("x_in")
        att_room = sem("att_room")
        vectors_in = sem("vectors_in")
        weights_in = sem("weights_in")
        att_ready = sem("att_ready")
        bias_ready = sem("bias_ready")
        h_ready = sem("h_ready")
        turned = sem("turned")
        turned_out = sem("turned_out")
        projected = sem("projected")
        parted = sem("parted")
        second = sem("second")
        q_ready = sem("q_ready")
        rest_ready = sem("rest_ready")
        q_used = sem("q_used")
        taken = sem("taken")
        self_scored = sem("self_scored")
        self_summed = sem("self_summed")
        acc_clear = sem("acc_clear")
        table_ready = sem("table_ready")
        table_out = sem("table_out")
        table_again = sem("table_again")
        merge_ready = sem("merge_ready")
        merge_exp = sem("merge_exp")
        merge_weights = sem("merge_weights")
        self_ready = sem("self_ready")
        stat_ready = sem("stat_ready")
        stat_sum = sem("stat_sum")
        x_again_room = sem("x_again_room")
        root_go = sem("root_go")
        root_done = sem("root_done")
        result_ready = sem("result_ready")
        result_out = sem("result_out")
        gathered = [sem(f"gathered{j}") for j in range(2 * NG)]
        idx_ready = sem("idx_ready")
        pool_go = sem("pool_go")
        loc_in = [sem(f"loc_in{j}") for j in range(2)]
        oht_ready = sem("oht_ready")
        z_ready = sem("z_ready")
        relu_ready = sem("relu_ready")
        scored = sem("scored")
        sm_v = sem("sm_v")
        sm_p = sem("sm_p")
        sm_a = sem("sm_a")
        row_pen = sem("row_pen")
        prepared = sem("prepared")
        columns = sem("columns")
        summed = sem("summed")
        flushed = sem("flushed")
        rescaled = sem("rescaled")

        block = ctx.enter_context(nc.Block())

        def area(which, width):
            o = which * AREA
            return ring[:, o:o + NB * width].rearrange("p (b f) -> p b f", b=NB)

        def turned_in(l):
            return ring[:, AREA:AREA + KC[l] * NB * P].rearrange("p (k n) -> p k n", k=KC[l])

        x_place = acc[:, :, 0:F]

        def layer_in(l, b, k):
            return x_place[:, b, :] if l == 0 else area(0, WR[l - 1])[:, b, k * P:k * P + KP[l]]

        def bank(b):
            return (ps_o[:, 0, :], ps_o[:, 1, :], ps_s[:, :, :].rearrange("p a b -> p (a b)"), ps_m[:, :])[b % 4]

        def prep(o, n, dt=F32):
            v = ring[:, o:o + n]
            return v if dt == F32 else v.bitcast(dt)

        TP = TG * P
        dst_l, dst_f, junk = prep(0, EROW, I32), prep(EROW, EROW), prep(2 * EROW, EROW)
        PR = 3 * EROW
        dst_r, src_r = prep(PR, TP, I32), prep(PR + TP, TP, I32)
        loc_w, valid, key_w, src_w = (prep(PR + k * TP, TP) for k in (2, 3, 4, 5))
        loc_bf = ring[:, PR + 6 * TP:PR + 6 * TP + TP // 2].bitcast(BF16)
        o = PR + 7 * TP
        ge, ged = prep(o, TG * (NB - 1)), prep(o + TG * (NB - 1), TG * (NB - 1))
        o += 2 * TG * (NB - 1)
        cnt, cnt_all, cmod, cdelta, cfloor, czero = (prep(o + k * (NB - 1), NB - 1) for k in range(6))
        o += 6 * (NB - 1)
        cint = prep(o, NB - 1, I32)
        o += NB - 1
        blk_f, run_f, blk128 = (prep(o + k * TG, TG) for k in range(3))
        o += 3 * TG
        blk_i, run_i = prep(o, TG, I32), prep(o + TG, TG, I32)
        key_t = [ring[:, k * NC * P:(k + 1) * NC * P].rearrange("p (c e) -> p c e", c=NC) for k in range(3)]
        o = 3 * NC * P
        first_key, last_key = ring[0:1, o:o + NT + 1], ring[0:1, o + NT + 1:o + 2 * (NT + 1)]
        o += 2 * (NT + 1)
        joined, cont = ring[0:1, o:o + NT], ring[0:1, o + NT:o + 2 * NT + 1]

        def rows(l, x2, t, n):
            s = (x2 * CT + t) * WR[l]
            return ring[:, s:s + n * WR[l]].rearrange("p (t w) -> p t w", t=n)

        def slots(c, old, new):
            def due(g):
                if g < LAG - NG:
                    return (shift(c, -2), g + 2 * NG - LAG) if old else None
                return (shift(c, -1), g + NG - LAG) if new else None
            return [(g, due(g - 1), due(g), due(g + 1)) for g in range(NG)]

        def edge_phase(eng, l, run):
            b = l * NC
            for c, scores, softmax, old, new in ((b, True, False, False, False), (b + 1, True, True, False, True)):
                run((None, c), scores, softmax, slots((None, c), old, new))
            with eng.Fori(0, NC // 2 - 1) as i:
                for k in (2, 3):
                    run((i, b + k), True, True, slots((i, b + k), True, True))
            for c, scores, softmax, old, new in ((b + NC, False, True, True, True), (b + NC + 1, False, False, True, False)):
                run((None, c), scores, softmax, slots((None, c), old, new))

        def blocks_of(eng, l, c, t, n):
            _, v = nc.values_load_multi_w_load_instructions(
                block_row[0:1, bass.ds(local(l, c, CT, t + 1), n)], engines={eng.engine}, min_val=0, max_val=NB - 1,
                skip_runtime_bounds_check_because="a count of block ends not after the tile, of NB - 1 in all")
            return v

        def y_root(q):
            return tiny[:, 6:7] if q == 0 else small[:, 4, 0:NB]

        def par(c):
            return c[1] % 2

        def local(l, c, a, b):
            return lin(shift(c, -l * NC), a, b)

        def at_least(eng, s, value):
            if not isinstance(value, int) or value > 0:
                eng.wait_ge(s, value)

        def broadcast(v, n=P):
            return v.rearrange("(o f) -> o f", o=1).partition_broadcast(n)[:, 0, :]

        @block.sync
        def _(sp):
            sp.dma_start(dst_l[0:EDIV, :], dst.rearrange("(p e) -> p e", p=EDIV)).then_inc(dst_in, 16)
            full = E // P * P
            n_pad = 0
            sp.wait_ge(const_ready, 1)
            for a, v, k in ((dst_d, dst, 0), (src_d, src, 1)):
                flat = a.rearrange("r e -> (r e)")
                sp.dma_start(a[0:E // P, :], v[0:full].rearrange("(r e) -> r e", e=P)).then_inc(padded, 16)
                if E > full:
                    sp.dma_start(flat[full:E].rearrange("(r e) -> r e", r=1),
                                 v[full:E].rearrange("(r e) -> r e", r=1)).then_inc(padded, 16)
                    n_pad += 1
                sp.dma_start(flat[E:E + NPAD].rearrange("(r e) -> r e", r=1), pads[0:1, k, :]).then_inc(padded, 16)
            for a in (0, (TG * P + 1) * P):
                sp.dma_start(key_d[a:a + P].rearrange("(r e) -> r e", r=1), fpad[0:1, :]).then_inc(stored, 16)
            with nc.allow_non_contiguous_dma(reason="one word per tile, once"):
                sp.wait_ge(keys_ready, 1)
                sp.dma_start(key_d[P:(TG * P + 1) * P].rearrange("(g p e) -> p g e", p=P, e=P),
                             key_w.rearrange("p (g e) -> p g e", g=TG)).then_inc(stored, 16)
                for g in range(TG):
                    r = min(P, NT - g * P)
                    sp.dma_start(loc_d[g * P:g * P + r, :], loc_bf[0:r, g * P:(g + 1) * P]).then_inc(stored, 16)
                sp.dma_start(loc_d[NT:NT + 2 * GT, :], loc_bf[0:2 * GT, 0:P]).then_inc(stored, 16)
                sp.dma_start(blk_d.rearrange("(g p) -> p g", p=P), blk_i).then_inc(stored, 16)
                sp.wait_ge(stored, (5 + TG) * 16)
                sp.wait_ge(prep_taken, 1)
                sp.dma_start(block_row[:, 1:NT + 1], blk_d[0:NT].rearrange("(o t) -> o t", o=1)).then_inc(keys_in, 16)
                for j, s in enumerate((0, -1, 1)):
                    view = key_d[P + s:P + s + NT * P].rearrange("(c t e) -> t c e", t=CT, e=P)
                    for h in range(HMAX):
                        sp.dma_start(key_t[j][h * CT:(h + 1) * CT, :, :], view).then_inc(keys_in, 16)
                sp.dma_start(first_key, key_d[P:(NT + 2) * P].rearrange("(o t e) -> o t e", o=1, e=P)[:, :, 0]).then_inc(keys_in, 16)
                sp.dma_start(last_key, key_d[0:(NT + 1) * P].rearrange("(o t e) -> o t e", o=1, e=P)[:, :, P - 1]).then_inc(keys_in, 16)

            sp.wait_ge(x_room, 1)
            sp.dma_start(x_place[:, 0:NB - 1, :], x[0:(NB - 1) * P, :].rearrange("(b p) f -> p b f", p=P)).then_inc(x_in, 16)
            sp.dma_start(x_place[0:LASTN, NB - 1, :], x[(NB - 1) * P:N, :]).then_inc(x_in, 16)

            def load_vectors(l):
                lay = layers[l]
                for q, name in enumerate(("bl", "br")):
                    sp.dma_start(bias_in[:, q * FS[l]:(q + 1) * FS[l]], broadcast(lay[name], PARTS)).then_inc(vectors_in, 16)
                sp.dma_start(att_hi[:, 0:FS[l]], broadcast(lay["att"].rearrange("h f -> (h f)"))).then_inc(vectors_in, 16)

            def load_weights(l):
                lay = layers[l]
                if l > 0:
                    sp.wait_ge(prepared, l * NC * NG)
                for q, name in enumerate(("Wl", "Wr")):
                    for k in range(KC[l]):
                        sp.dma_start(weights[0:KP[l], k, q * FS[l]:(q + 1) * FS[l]],
                                     lay[name][k * P:k * P + KP[l], :]).then_inc(weights_in, 16)
                with nc.allow_non_contiguous_dma(reason="a column of attention weights"):
                    for h in range(HS[l]):
                        a = h * F % P
                        sp.dma_start(att_bd[a:a + F, h * F // P, h:h + 1],
                                     lay["att"][h, :].rearrange("(f o) -> f o", o=1)).then_inc(weights_in, 16)

            def local_destinations(l, c, j):
                at_least(sp, oht_ready, lin(c, NG // 2, j - 1))
                sp.dma_start(locbc[:, j % 2, :],
                             loc_d[bass.ds(local(l, c, CT, j * 2 * GT), 2 * GT), :]
                             .rearrange("t e -> (t e)").rearrange("(o f) -> o f", o=1).partition_broadcast(P)[:, 0, :]
                             ).then_inc(loc_in[j % 2], 16)

            sp.wait_ge(att_room, 1)
            load_vectors(0)
            for l in range(NL):
                load_weights(l)
                for q in range(MG):
                    b0, b1 = STARTS[q], STARTS[q + 1]
                    sp.wait_ge(table_ready, l * MG + q + 1)
                    sp.dma_start(table[l][b0 * P:b1 * P, :].rearrange("(b p) f -> p b f", p=P),
                                 area(0, WR[l])[:, b0:b1, :]).then_inc(table_out, 16)
                sp.dma_start(bias_out[:, 0:FS[l]], broadcast(layers[l]["bias"])).then_inc(bias_ready, 16)
                if l == 0:
                    local_destinations(0, (None, 0), 0)
                for c in range(2):
                    for j in range(1, NG // 2 + 1):
                        local_destinations(l, (None, l * NC + c), j)
                with sp.Fori(0, NC // 2 - 1) as i:
                    for k in (2, 3):
                        for j in range(1, NG // 2 + 1):
                            local_destinations(l, (i, l * NC + k), j)
                sp.wait_ge(prepared, (l + 1) * NC * NG - NG)
                if l < NL - 1:
                    load_vectors(l + 1)
                sp.dma_start(area(0, WR[l]), table[l].rearrange("(b p) f -> p b f", p=P)).then_inc(table_again, 16)
            sp.wait_ge(x_again_room, 1)
            sp.dma_start(x_place[:, 0:NB - 1, :], x[0:(NB - 1) * P, :].rearrange("(b p) f -> p b f", p=P)).then_inc(x_in, 16)
            sp.dma_start(x_place[0:LASTN, NB - 1, :], x[(NB - 1) * P:N, :]).then_inc(x_in, 16)
            sp.dma_start(lnw[:, 0, :], broadcast(ln_w)).then_inc(x_in, 16)
            sp.dma_start(lnw[:, 1, :], broadcast(ln_b)).then_inc(x_in, 16)
            sp.wait_ge(result_ready, 1)
            sp.dma_start(out[0:(NB - 1) * P, :].rearrange("(b p) f -> p b f", p=P),
                         area(1, F)[:, 0:NB - 1, :]).then_inc(result_out, 16)
            sp.dma_start(out[(NB - 1) * P:N, :], area(1, F)[0:LASTN, NB - 1, :]).then_inc(result_out, 16)
            sp.wait_ge(result_out, 32)

        @block.gpsimd
        def _(pool):
            n = [0]

            def link(ins):
                n[0] += 1
                ins.then_inc(pool_own, 1)
                pool.wait_ge(pool_own, n[0])

            pool.memset(pads[:, 1, :], 0)
            pool.memset(fpad[:, :], -5.0)
            link(pool.memset(pads[:, 0, :], -1))
            pool.sem_inc(const_ready, 1)
            pool.iota(iota_row[:, :], pattern=[[1, P]], base=0, channel_multiplier=0, allow_small_or_imprecise_dtypes=True)
            pool.iota(iota_col[:, :], pattern=[[0, 1]], base=0, channel_multiplier=1, allow_small_or_imprecise_dtypes=True)
            pool.iota(tile_no[:, :], pattern=[[P, TG]], base=0, channel_multiplier=1, allow_small_or_imprecise_dtypes=True)
            pool.memset(ones[:, :], 1.0)
            pool.memset(ones_rows[:, :], 1.0)
            pool.memset(node_mask[:, :], 1.0)
            link(pool.memset(ident[:, :], 0.0))
            pool.affine_select(out=ident[:, :], in_=ident[:, :], compare_op=ALU.not_equal, fill=1.0, base=0,
                               pattern=[[-1, P]], channel_multiplier=1)
            link(pool.affine_select(out=node_mask[:, :], in_=node_mask[:, :], compare_op=ALU.is_ge, fill=0.0,
                                    base=N - 1, pattern=[[-P, NB]], channel_multiplier=-1))
            pool.sem_inc(const_ready, 1)

            pool.wait_ge(padded, 16 * (4 + 2 * (E % P > 0)))
            pool.wait_ge(runs_ready, 1)
            for g in range(TG):
                for a, r in ((dst_d, dst_r), (src_d, src_r)):
                    pool.indirect_dma_start(r[:, g * P:(g + 1) * P], None, a[:, :],
                                            bass.IndirectOffsetOnAxis(ap=run_i[:, g:g + 1], axis=0)).then_inc(rows_in, 16)

            def gather(l, c, first):
                x2 = par(c)
                if not first:
                    pool.wait_ge(scored, lin(c, NG, -NG))
                pool.tensor_copy(idx[:, x2, :], src_e[:, bass.ds(local(l, c, CT, 0), CT)]).then_inc(idx_ready, 1)
                pool.wait_ge(idx_ready, lin(c, 1, 1))
                for g in range(NG):
                    at_least(pool, prepared, lin(c, NG, g + 1 - 2 * NG))
                    pool.sem_inc(pool_go, 1)
                    for k in range(GT):
                        t = g * GT + k
                        pool.indirect_dma_start(rows(l, x2, t, 1)[:, 0, :], None, table[l][:, :],
                                                bass.IndirectOffsetOnAxis(ap=idx[:, x2, t:t + 1], axis=0)
                                                ).then_inc(gathered[x2 * NG + g], 16)

            def node_phase(l):
                fs = FS[l]
                pool.wait_ge(vectors_in, V_DMAS * (l + 1))
                pool.tensor_scalar(att_lo[:, 0:fs], att_hi[:, 0:fs], SLOPE_ATT, None, ALU.mult)
                link(pool.tensor_copy(bias_part[:, 0, 0:2 * fs], bias_in[:, 0:2 * fs]))
                pool.tensor_scalar(att_hi[:, 0:fs], att_hi[:, 0:fs], 1.0 - SLOPE_ATT, None, ALU.mult)
                link(pool.tensor_tensor(bias_rest[:, 0:2 * fs], bias_in[:, 0:2 * fs], bias_part[:, 0, 0:2 * fs], ALU.subtract))
                link(pool.tensor_copy(bias_part[:, 1, 0:2 * fs], bias_rest[:, 0:2 * fs]))
                link(pool.tensor_tensor(bias_rest[:, 0:2 * fs], bias_rest[:, 0:2 * fs], bias_part[:, 1, 0:2 * fs], ALU.subtract))
                pool.tensor_scalar(bias_rest[:, 0:2 * fs], bias_rest[:, 0:2 * fs], ident[0:PARTS, 2:3], None, ALU.mult)
                link(pool.tensor_scalar(bias_part[:, 0, 0:2 * fs], bias_part[:, 0, 0:2 * fs], ident[0:PARTS, 0:1], None, ALU.mult))
                link(pool.tensor_scalar(bias_part[:, 1, 0:2 * fs], bias_part[:, 1, 0:2 * fs], ident[0:PARTS, 1:2], None, ALU.mult))
                link(pool.tensor_tensor(bias_part[:, 0, 0:2 * fs], bias_part[:, 0, 0:2 * fs], bias_part[:, 1, 0:2 * fs], ALU.add))
                link(pool.tensor_tensor(bias_rows[:, 0:2 * fs], bias_part[:, 0, 0:2 * fs], bias_rest[:, 0:2 * fs], ALU.add))
                pool.wait_ge(weights_in, W_DMAS[l])
                link(pool.tensor_scalar(att_bd[:, :, :], att_bd[:, :, :], 1.0 - SLOPE_ATT, None, ALU.mult))
                pool.sem_inc(att_ready, 1)
                if l > 0:
                    merge(l - 1, 0)
                for b in range(NB):
                    if l > 0 and b == STARTS[group_of[b]] and group_of[b] + 1 < MG:
                        merge(l - 1, group_of[b] + 1)
                    if b > 0 and b == STARTS[group_of[b]]:
                        clear(l, group_of[b] - 1)
                    pool.wait_ge(parted, l * NB + b + 1)
                    if l * NB + b >= 2:
                        pool.wait_ge(q_used, l * NB + b - 1)
                    pool.tensor_tensor(tmp[:, 3 + b % 2, 0:fs], area(0, WR[l])[:, b, 0:fs], att_lo[:, 0:fs],
                                       ALU.mult).then_inc(q_ready, 1)
                clear(l, MG - 1)

            def clear(l, q):
                pool.wait_ge(turned, l * NB + STARTS[q + 1])
                pool.memset(acc[:, STARTS[q]:STARTS[q + 1], :], 0.0).then_inc(acc_clear, 1)

            def merge(l, q):
                hh = HS[l]
                if q == 0:
                    pool.wait_ge(table_again, 16 * (l + 1))
                    pool.wait_ge(merge_weights, l + 1)
                b0, b1 = STARTS[q], STARTS[q + 1]
                xs = area(0, WR[l])[:, b0:b1, 0:FS[l]].rearrange("p b (h f) -> p b h f", h=hh)
                w = small[:, 7, :].rearrange("p (b h) -> p b h", b=NB)[:, b0:b1, 0:hh]
                pool.tensor_tensor(xs, xs, w.unsqueeze(3).broadcast_to([P, b1 - b0, hh, F]), ALU.mult).then_inc(self_ready, 1)

            for l in range(NL):
                if l == 0:
                    pool.wait_ge(lists_ready, 1)
                node_phase(l)
                pool.wait_ge(table_out, 16 * MG * (l + 1))
                for c in range(2):
                    gather(l, (None, l * NC + c), l == 0)
                with pool.Fori(0, NC // 2 - 1) as i:
                    for k in (2, 3):
                        gather(l, (i, l * NC + k), False)
            for q in range(MG):
                merge(NL - 1, q)

        @block.scalar
        def _(act):
            def relu(l, c, g):
                v = lin(c, NG, g)
                act.wait_ge(z_ready, lin(c, NG, g + 1))
                at_least(act, scored, lin(c, NG, g - 1))
                nk = FP[l] // P
                act.activation(relu_z[:, g % 2, :, 0:nk, :],
                               ps_z[:, g % 2, :, :].rearrange("p a b -> p (a b)")[:, 0:GT * nk * P]
                               .rearrange("p (t k e) -> p t k e", t=GT, k=nk), ACT.Relu).then_inc(relu_ready, 1)

            def exponentials(l, c):
                act.wait_ge(sm_v, lin(c, SV, 17))
                act.activation(prob_t[:, :], shifted[:, :], ACT.Exp).then_inc(sm_a, 1)
                act.activation(rescale[:, :], carry_col[:, 2:], ACT.Exp).then_inc(sm_a, 1)

            def per_edge(l, c):
                act.wait_ge(sm_p, lin(c, SP_, 4))
                for d, o in ((prob_e, PM_PROB), (max_e, PM_MAX)):
                    act.activation(d[:, par(c), :, :], ps_m[:, o:o + P].rearrange("p (h t) -> p t h", h=HMAX),
                                   ACT.Copy).then_inc(sm_a, 1)

            def row_penalties(l, c):
                at_least(act, sm_v, lin(c, SV, 7 - SV))
                for d, v in ((heads_pen_f[:, :, 1:CT + 1], row_pen_f), (heads_pen_b[:, :, :], row_pen_b)):
                    ins = act.activation(d, v[:, bass.ds(local(l, c, 1, 0), 1), :].broadcast_to([1, HMAX, CT]), ACT.Copy)
                ins.then_inc(row_pen, 1)

            def weight_columns(l, c, g):
                h = HS[l]
                w = weighted[:, g % 2, :, :]
                act.wait_ge(sm_a, lin(c, SA, 4))
                at_least(act, summed, lin(c, CT, GT * (g - 1)))
                t = slice(g * GT, (g + 1) * GT)
                act.activation(w[:, :, 0:h * (F + 1)].rearrange("p t (h f) -> p t h f", h=h)[:, :, :, F],
                               prob_e[:, par(c), t, 0:h], ACT.Copy)
                act.activation(w[:, :, h * (F + 1):h * (F + 2)], max_e[:, par(c), t, 0:h],
                               ACT.Copy).then_inc(columns, 1)

            def run_chunk(l):
                def run(c, scores, soft, plan):
                    for g, _, _, ahead in plan:
                        if soft and g == 5:
                            per_edge(l, shift(c, -1))
                        if scores and g > 0:
                            relu(l, c, g - 1)
                        if soft and g == 0:
                            relu(l, shift(c, -1), NG - 1)
                            row_penalties(l, shift(c, -1))
                        if ahead:
                            weight_columns(l, *ahead)
                        if soft and g == 4:
                            exponentials(l, shift(c, -1))
                return run

            act.wait_ge(lists_ready, 1)
            for l in range(NL):
                for b in range(NB + 2):
                    if b < NB:
                        act.wait_ge(turned, l * NB + b + 1)
                        act.activation(turned_in(l)[0:KP[l], :, b * P:(b + 1) * P],
                                       ps_z[0:KP[l], b % 4 // 2, b % 2, 0:KC[l] * P].rearrange("p (k n) -> p k n", k=KC[l]),
                                       ACT.Copy).then_inc(turned_out, 1)
                    if b >= 1 and b <= NB:
                        act.wait_ge(projected, l * NB + b)
                        act.activation(area(0, WR[l])[:, b - 1, 0:FS[l]], bank(b - 1)[:, 0:FS[l]], ACT.Copy)
                        act.activation(xr_parts[:, 0, b - 1, 0:FS[l]], bank(b - 1)[:, FS[l]:2 * FS[l]], ACT.Copy).then_inc(parted, 1)
                    if b >= 2:
                        act.wait_ge(rest_ready, l * NB + b - 1)
                        act.activation(xr_parts[:, 1, b - 2, 0:FS[l]], tmp[:, 5 + (b - 2) % 3, 0:FS[l]], ACT.Copy).then_inc(second, 1)
                edge_phase(act, l, run_chunk(l))
                act.wait_ge(merge_ready, l + 1)
                for k in (2, 3):
                    ins = act.activation(small[:, k, :], small[:, k, :], ACT.Exp)
                ins.then_inc(merge_exp, 1)
            for q, v in enumerate((tiny[:, 3:4], small[:, 2, 0:NB])):
                act.wait_ge(root_go, q + 1)
                act.activation(y_root(q), v, ACT.Sqrt).then_inc(root_done, 1)

        @block.tensor
        def _(pe):
            pe.wait_ge(const_ready, 2)
            pe.wait_ge(counts_ready, 1)
            pe.matmul(ps_m[:, 0:NB - 1], ones[0:EDIV, :], cnt[0:EDIV, :], start=True, stop=True).then_inc(counts_sum, 1)
            pe.wait_ge(keys_ready, 1)
            for g in range(TG):
                if g >= 2:
                    pe.wait_ge(taken, g - 1)
                for k, w in enumerate((loc_w, src_w)):
                    ins = pe.transpose(ps_o[:, g % 2, k * P:(k + 1) * P], w[:, g * P:(g + 1) * P], ident[:, :])
                ins.then_inc(prep_turned, 1)

            def z_tile(l, c, g, k, blk, scores_of):
                x2, nk = par(c), FP[l] // P
                z = ps_z[:, g % 2, :, :].rearrange("p a b -> p (a b)")
                zk = [z[:, (k * nk + q) * P:(k * nk + q + 1) * P] for q in range(nk)]
                t = g * GT + k
                if k == 0:
                    pe.wait_ge(gathered[x2 * NG + g], lin(c, 32, 64 - 32 * x2))
                for q in range(nk):
                    pe.matmul(zk[q], rows(l, x2, t, 1)[:, 0, q * P:(q + 1) * P], ident[:, :],
                              is_transpose=True, start=(q == 0), stop=False)
                if scores_of:
                    for j in (((), (0,), (1,), (2, 3)) if nk > 1 else ((), (), (), (0, 1, 2, 3)))[k]:
                        score_tile(l, *scores_of, j)
                if g % 2 == 0 and k == 0:
                    pe.wait_ge(oht_ready, lin(c, NG // 2, g // 2 + 1))
                for q in range(nk):
                    for r in range(PARTS):
                        ins = pe.matmul(zk[q], xr_parts[:, r, bass.ds(blk, 1), q * P:(q + 1) * P].rearrange("p b f -> p (b f)"),
                                        oht[:, g // 2 % 2, (g % 2 * GT + k) * P:(g % 2 * GT + k + 1) * P],
                                        start=False, stop=(r == PARTS - 1 and q == nk - 1))
                if k == GT - 1:
                    ins.then_inc(z_ready, 1)

            def score_tile(l, c, g, k):
                h, nk = HS[l], FP[l] // P
                if k == 0:
                    if g == 0 and not (c[0] is None and c[1] == l * NC):
                        pe.wait_ge(sm_v, lin(shift(c, -1), SV, 1))
                    pe.wait_ge(relu_ready, lin(c, NG, g + 1))
                s = ps_s[:, par(c), g * GT + k:g * GT + k + (h - 1) * CT + 1:CT]
                for q in range(nk):
                    ins = pe.matmul(s, relu_z[:, g % 2, k, q, :], att_bd[:, q, 0:h], start=(q == 0), stop=(q == nk - 1))
                if k == GT - 1:
                    ins.then_inc(scored, 1)

            def softmax(l, c, step):
                pe.wait_ge(sm_v, lin(c, SV, (1, 3, 12, 18)[step]))
                if step == 0:
                    at_least(pe, sm_a, lin(c, SA, 0))
                    ins = pe.transpose(ps_m[:, PM_T:PM_T + P], score[:, :], ident[:, :])
                elif step == 1:
                    pe.transpose(ps_m[0:1, PM_L:PM_L + P], run_fwd[:, P - 1:P], ident[:, :])
                    ins = pe.transpose(ps_m[0:1, PM_F:PM_F + P], run_bwd[:, 0:1], ident[:, :])
                elif step == 2:
                    for q, v in enumerate((carry_f, carry_b)):
                        pe.matmul(ps_m[:, PM_C + q:PM_C + q + 1], v[:, :, :].rearrange("o h t -> o (h t)"),
                                  ones[0:1, 0:1], start=True, stop=True)
                    ins = pe.matmul(ps_m[:, PM_B:PM_B + HMAX], first_hot[:, :], boundary[:, 1, :], start=True, stop=True)
                else:
                    pe.wait_ge(sm_a, lin(c, SA, 1))
                    pe.transpose(ps_m[:, PM_PROB:PM_PROB + P], prob_t[:, :], ident[:, :])
                    ins = pe.transpose(ps_m[:, PM_MAX:PM_MAX + P], max_last[:, :], ident[:, :])
                ins.then_inc(sm_p, 1)

            def sum_tile(l, c, g, k):
                if k == 0:
                    pe.wait_ge(columns, lin(c, NG, g + 1))
                    pe.wait_ge(prepared, lin(c, NG, g + 1))
                at_least(pe, flushed, lin(c, CT, g * GT + k - 1))
                pe.matmul(ps_o[:, k % 2, 0:WS[l]], oh[:, g % 2, k, :], weighted[:, g % 2, k, 0:WS[l]],
                          start=True, stop=True).then_inc(summed, 1)

            def run_chunk(l):
                def run(c, scores, soft, plan):
                    for g, _, sums, _ in plan:
                        scores_of = (c, g - 1) if g > 0 and scores else (shift(c, -1), NG - 1) if g == 0 and soft else None
                        if scores:
                            blks = blocks_of(pe, l, c, g * GT, GT)
                        for k in range(GT):
                            if scores:
                                z_tile(l, c, g, k, blks[k], scores_of)
                            elif scores_of:
                                score_tile(l, *scores_of, k)
                            if sums:
                                sum_tile(l, *sums, k)
                        if soft and 0 < g <= SP_:
                            softmax(l, shift(c, -1), g - 1)
                return run

            def total(q):
                pe.wait_ge(stat_ready, q + 1)
                pe.matmul(ps_m[:, q:q + 1], ones[:, :], tiny[:, q:q + 1], start=True, stop=True).then_inc(stat_sum, 1)

            for l in range(NL):
                if l == 0:
                    pe.wait_ge(x_in, 32)
                pe.wait_ge(att_ready, l + 1)
                for b in range(NB + 1):
                    if b < NB:
                        if b == STARTS[group_of[b]]:
                            pe.wait_ge(h_ready, l * MG + group_of[b] + 1)
                        at_least(pe, turned_out, l * NB + b - 3 if b >= 4 else 0)
                        for k in range(KC[l]):
                            ins = pe.transpose(ps_z[0:KP[l], b % 4 // 2, b % 2, k * P:(k + 1) * P],
                                               layer_in(l, b, k), ident[:, :])
                        ins.then_inc(turned, 1)
                    if b == 0:
                        pe.wait_ge(taken, TG)
                        continue
                    a = b - 1
                    pe.wait_ge(turned_out, l * NB + a + 1)
                    if a >= 4:
                        pe.wait_ge(rest_ready, l * NB + a - 3)
                    z = bank(a)[:, 0:2 * FS[l]]
                    for k in range(KC[l]):
                        pe.matmul(z, turned_in(l)[0:KP[l], k, a * P:(a + 1) * P],
                                  weights[0:KP[l], k, 0:2 * FS[l]], start=(k == 0), stop=False)
                    pe.matmul(z, ones_rows[:, :], bias_rows[:, 0:2 * FS[l]], start=False, stop=True).then_inc(projected, 1)
                edge_phase(pe, l, run_chunk(l))
            total(0)
            total(1)

        @block.vector
        def _(dve):
            n = [0]

            def link(ins):
                n[0] += 1
                ins.then_inc(dve_own, 1)
                dve.wait_ge(dve_own, n[0])

            dve.memset(acc[:, :, :], 0.0)
            dve.memset(run_row[:, :, :], -BIG)
            dve.memset(score[:, :], 0.0)
            dve.memset(heads_pen_f[:, :, :], -BIG)
            dve.memset(row_pen_b[:, :, :], -BIG)
            dve.memset(carry_pen_b[:, :, :], -BIG)
            dve.memset(czero, 0.0)
            dve.memset(block_row[:, 0:1], 0)
            link(dve.memset(carry_b[:, :, :], -BIG))
            dve.sem_inc(x_room, 1)
            dve.sem_inc(h_ready, MG)

            dve.wait_ge(dst_in, 16)
            link(dve.tensor_copy(dst_f[0:EDIV, :], dst_l[0:EDIV, :]))
            for b in range(1, NB):
                link(dve.tensor_scalar(junk[0:EDIV, :], dst_f[0:EDIV, :], float(b * P), None, ALU.is_lt))
                link(dve.tensor_reduce(cnt[0:EDIV, b - 1:b], junk[0:EDIV, :], AX.X, ALU.add))
            dve.sem_inc(counts_ready, 1)
            dve.wait_ge(counts_sum, 1)
            link(dve.tensor_copy(cnt_all, ps_m[:, 0:NB - 1]))
            link(dve.tensor_copy(cint, cnt_all))
            link(dve.tensor_scalar(cint, cint, P.bit_length() - 1, None, ALU.arith_shift_right))
            link(dve.tensor_copy(cfloor, cint))
            link(dve.tensor_scalar(cmod, cfloor, float(P), None, ALU.mult))
            link(dve.tensor_tensor(cdelta, cnt_all, cmod, ALU.is_gt))
            link(dve.tensor_tensor_scan(cmod, cdelta, czero, 0.0, ALU.add, ALU.add))
            link(dve.tensor_tensor(cfloor, cfloor, cmod, ALU.add))
            dve.wait_ge(const_ready, 2)
            ge3 = ge.rearrange("p (g b) -> p g b", g=TG)
            ged3 = ged.rearrange("p (g b) -> p g b", g=TG)

            def wide(v):
                return v.unsqueeze(1).broadcast_to([P, TG, NB - 1])

            link(dve.tensor_tensor(ge3, tile_no[:, :].unsqueeze(2).broadcast_to([P, TG, NB - 1]), wide(cfloor), ALU.is_ge))
            link(dve.tensor_tensor(ged3, ge3, wide(cdelta), ALU.mult))
            link(dve.tensor_reduce(blk_f, ge3, AX.X, ALU.add))
            link(dve.tensor_reduce(run_f, ged3, AX.X, ALU.add))
            link(dve.tensor_tensor(run_f, tile_no[:, :], run_f, ALU.subtract))
            link(dve.tensor_scalar(run_i, run_f, float(OT), None, ALU.min))
            dve.sem_inc(runs_ready, 1)
            link(dve.tensor_copy(blk_i, blk_f))
            link(dve.tensor_scalar(blk128, blk_f, float(P), None, ALU.mult))
            dve.wait_ge(rows_in, 16 * 2 * TG)
            dst3, loc3 = (v.rearrange("p (g e) -> p g e", g=TG) for v in (dst_r, loc_w))
            link(dve.tensor_tensor(loc3, dst3, blk128.unsqueeze(2).broadcast_to([P, TG, P]), ALU.subtract))
            link(dve.tensor_scalar(valid, loc_w, 0.0, None, ALU.is_ge))
            link(dve.tensor_scalar(key_w, loc_w, float(P), None, ALU.is_lt))
            link(dve.tensor_tensor(valid, valid, key_w, ALU.mult))
            link(dve.tensor_scalar(key_w, dst_r, 1.0, None, ALU.add))
            link(dve.tensor_tensor(key_w, key_w, valid, ALU.mult))
            link(dve.tensor_scalar(loc_w, loc_w, 1.0, None, ALU.add))
            link(dve.tensor_tensor(loc_w, loc_w, valid, ALU.mult))
            link(dve.tensor_scalar(loc_w, loc_w, -1.0, None, ALU.add))
            link(dve.tensor_copy(loc_bf, loc_w))
            link(dve.tensor_copy(src_w, src_r))
            dve.sem_inc(keys_ready, 1)
            for g in range(TG):
                dve.wait_ge(prep_turned, g + 1)
                dve.tensor_copy(loc_e[:, g * P:(g + 1) * P], ps_o[:, g % 2, 0:P])
                link(dve.tensor_copy(src_e[:, g * P:(g + 1) * P], ps_o[:, g % 2, P:2 * P]))
                dve.sem_inc(taken, 1)
            dve.sem_inc(prep_taken, 1)
            dve.wait_ge(keys_in, 16 * (1 + 3 * HMAX + 2))
            link(dve.tensor_tensor(key_t[1], key_t[0], key_t[1], ALU.not_equal))
            link(dve.tensor_scalar(pen_f[:, :, :], key_t[1], -BIG, None, ALU.mult))
            link(dve.tensor_tensor(key_t[2], key_t[0], key_t[2], ALU.not_equal))
            link(dve.tensor_scalar(pen_b[:, :, ::-1], key_t[2], -BIG, None, ALU.mult))
            link(dve.tensor_tensor(cont, first_key, last_key, ALU.is_equal))
            link(dve.tensor_tensor(joined, first_key[:, 0:NT], last_key[:, 1:NT + 1], ALU.is_equal))

            def penalty(o, v):
                link(dve.tensor_scalar(o, v, -1.0, BIG, ALU.add, ALU.mult))

            cont_before = cont[:, 0:NT].rearrange("o (c t) -> o c t", t=CT)
            cont_after = cont[:, 1:NT + 1].rearrange("o (c t) -> o c t", t=CT)
            penalty(carry_pen_f[:, :, :], cont_before)
            penalty(carry_pen_b[:, :, 0:CT - 1], cont_after[:, :, 0:CT - 1])
            joined3 = joined.rearrange("o (c t) -> o c t", t=CT)
            both = first_key[:, 0:NT].rearrange("o (c t) -> o c t", t=CT)
            link(dve.tensor_tensor(both, joined3, cont_before, ALU.mult))
            penalty(row_pen_f[:, :, :], both)
            link(dve.tensor_tensor(both, joined3, cont_after, ALU.mult))
            penalty(row_pen_b[:, :, 0:CT - 1], both[:, :, 0:CT - 1])
            link(dve.tensor_copy(chunk_cont[:, :], cont_before[:, :, 0]))
            dve.sem_inc(lists_ready, 1)

            def node_phase(l):
                hh, fs = HS[l], FS[l]
                if l > 0:
                    merge_weights_of(l - 1)
                    merge(l - 1, 0)
                tab = area(0, WR[l])
                if FP[l] > fs:
                    dve.memset(xr_parts[:, :, :, fs:FP[l]], 0.0)
                dve.wait_ge(att_ready, l + 1)

                def heads(v):
                    return v.rearrange("p (h f) -> p h f", h=hh)

                for b in range(NB + 1):
                    z, rest = tmp[:, b % 3, 0:fs], tmp[:, 5 + b % 3, 0:fs]
                    if l > 0 and b < NB and b == STARTS[group_of[b]] and group_of[b] + 1 < MG:
                        merge(l - 1, group_of[b] + 1)
                    if b < NB:
                        xr = bank(b)[:, fs:2 * fs]
                        dve.wait_ge(parted, l * NB + b + 1)
                        if FP[l] > fs:
                            dve.memset(tab[:, b, fs:FP[l]], 0.0)
                        dve.tensor_tensor(z, tab[:, b, 0:fs], xr, ALU.add)
                        dve.tensor_tensor(rest, xr, xr_parts[:, 0, b, 0:fs], ALU.subtract).then_inc(rest_ready, 1)
                    if b > 0:
                        a = b - 1
                        dve.wait_ge(q_ready, l * NB + a + 1)
                        dve.tensor_reduce(tab[:, a, FP[l]:FP[l] + hh], heads(tmp[:, 3 + a % 2, 0:fs]), AX.X, ALU.add)
                        dve.wait_ge(second, l * NB + a + 1)
                        dve.tensor_tensor(xr_parts[:, 2, a, 0:fs], tmp[:, 5 + a % 3, 0:fs], xr_parts[:, 1, a, 0:fs],
                                          ALU.subtract).then_inc(q_used, 1)
                        dve.wait_ge(self_scored, l * NB + a + 1)
                        dve.tensor_reduce(s_self[:, a, 0:hh], heads(tmp[:, a % 3, 0:fs]), AX.X, ALU.add).then_inc(self_summed, 1)
                    if b < NB:
                        dve.wait_ge(rest_ready, l * NB + b + 1)
                        dve.scalar_tensor_tensor(out=z, in0=z, scalar=0.0, in1=att_hi[:, 0:fs], op0=ALU.max,
                                                 op1=ALU.mult).then_inc(self_scored, 1)
                    if b > 0:
                        if a == STARTS[group_of[a] + 1] - 1:
                            dve.wait_ge(self_summed, l * NB + a + 1)
                            g = slice(STARTS[group_of[a]], a + 1)
                            dve.tensor_tensor(s_self[:, g, 0:hh], s_self[:, g, 0:hh], tab[:, g, FP[l]:FP[l] + hh],
                                              ALU.add).then_inc(table_ready, 1)
                dve.wait_ge(acc_clear, (l + 1) * MG)

            def one_hot_t(l, c, j):
                dve.wait_ge(loc_in[j % 2], lin(c, 32, 16 * (j // 2 + 1)))
                at_least(dve, z_ready, lin(c, NG, 2 * j - 2))
                dve.tensor_scalar(oht[:, j % 2, :], locbc[:, j % 2, :], iota_col[:, 0:1], None,
                                  ALU.is_equal).then_inc(oht_ready, 1)

            def softmax(l, c, step):
                def done(k):
                    dve.wait_ge(sm_v, lin(c, SV, k))

                hh = HS[l]
                cl = local(l, c, 1, 0)

                def of_chunk(v):
                    return v[:, bass.ds(cl, 1)]

                def flat(v):
                    return v.rearrange("p c e -> p (c e)")

                turned_score = ps_m[:, PM_T:PM_T + P]
                if step == 0:
                    dve.wait_ge(scored, lin(c, NG, NG))
                    dve.tensor_tensor(score[:, 0:hh * CT].rearrange("p (h t) -> p h t", h=hh),
                                      ps_s[:, par(c), 0:hh * CT].rearrange("p (h t) -> p h t", h=hh),
                                      rows(l, par(c), 0, CT)[:, :, FP[l]:FP[l] + hh].rearrange("p t h -> p h t"),
                                      ALU.add).then_inc(sm_v, 1)
                elif step == 1:
                    dve.wait_ge(sm_p, lin(c, SP_, 1))
                    dve.tensor_tensor_scan(run_fwd[:, :], flat(of_chunk(pen_f)), turned_score, -BIG,
                                           ALU.add, ALU.max).then_inc(sm_v, 1)
                    dve.tensor_tensor_scan(run_bwd[:, ::-1], flat(of_chunk(pen_b)), turned_score[:, ::-1],
                                           -BIG, ALU.add, ALU.max).then_inc(sm_v, 1)
                elif step == 2:
                    dve.wait_ge(sm_p, lin(c, SP_, 2))
                    dve.tensor_copy(run_in[:, :, 1:CT + 1], ps_m[0:1, PM_L:PM_L + P].rearrange("o (h t) -> o h t", h=HMAX)
                                    ).then_inc(sm_v, 1)
                    dve.tensor_copy(run_in[:, :, 0:1], run_row[:, :, CT:CT + 1]).then_inc(sm_v, 1)
                    done(5)
                    dve.wait_ge(row_pen, lin(c, 1, 1))
                    dve.tensor_tensor_scan(run_row[:, :, :].rearrange("o h t -> o (h t)"),
                                           heads_pen_f[:, :, :].rearrange("o h t -> o (h t)"),
                                           run_in[:, :, :].rearrange("o h t -> o (h t)"), -BIG,
                                           ALU.add, ALU.max).then_inc(sm_v, 1)
                    dve.tensor_tensor_scan(back_row[:, :, :].rearrange("o h t -> o (h t)")[:, ::-1],
                                           heads_pen_b[:, :, :].rearrange("o h t -> o (h t)")[:, ::-1],
                                           ps_m[0:1, PM_F:PM_F + P][:, ::-1], -BIG,
                                           ALU.add, ALU.max).then_inc(sm_v, 1)
                    done(6)
                    dve.tensor_tensor(carry_f[:, :, :], run_row[:, :, 0:CT],
                                      of_chunk(carry_pen_f).broadcast_to([1, HMAX, CT]), ALU.add).then_inc(sm_v, 1)
                    done(7)
                    dve.tensor_tensor(carry_b[:, :, 0:CT - 1], back_row[:, :, 1:CT],
                                      of_chunk(carry_pen_b)[:, :, 0:CT - 1].broadcast_to([1, HMAX, CT - 1]),
                                      ALU.add).then_inc(sm_v, 1)
                    dve.tensor_tensor(boundary[:, 0, :], run_in[:, :, 0], back_row[:, :, 0],
                                      ALU.subtract).then_inc(sm_v, 1)
                    done(10)
                    dve.tensor_scalar(boundary[:, 1, :], boundary[:, 0, :], 0.0, chunk_cont[:, bass.ds(cl, 1)],
                                      ALU.min, ALU.mult).then_inc(sm_v, 1)
                    dve.tensor_scalar(first_hot[:, :], iota_row[0:1, :], loc_e[0:1, bass.ds(local(l, c, CT, 0), 1)], None,
                                      ALU.is_equal).then_inc(sm_v, 1)
                else:
                    dve.wait_ge(sm_p, lin(c, SP_, 3))
                    dve.tensor_copy(carry_col[:, :], ps_m[:, PM_C:PM_B + HMAX]).then_inc(sm_v, 1)
                    done(13)
                    dve.tensor_tensor_scan(run_fwd[:, :], flat(of_chunk(pen_f)), turned_score, carry_col[:, 0:1],
                                           ALU.add, ALU.max).then_inc(sm_v, 1)
                    dve.tensor_tensor_scan(run_bwd[:, ::-1], flat(of_chunk(pen_b)), turned_score[:, ::-1],
                                           carry_col[:, 1:2], ALU.add, ALU.max).then_inc(sm_v, 1)
                    done(15)
                    dve.tensor_tensor(edge_max[:, :], run_fwd[:, :], run_bwd[:, :], ALU.max).then_inc(sm_v, 1)
                    done(16)
                    dve.tensor_tensor(shifted[:, :], turned_score, edge_max[:, :], ALU.subtract).then_inc(sm_v, 1)
                    dve.scalar_tensor_tensor(out=max_last[:, ::-1], in0=flat(of_chunk(pen_b)), scalar=-1.0 / BIG,
                                             in1=edge_max[:, ::-1], op0=ALU.mult, op1=ALU.mult).then_inc(sm_v, 1)

            def one_hot(l, c, g):
                dve.tensor_tensor(oh[:, g % 2, :, :], iota_row[:, :].unsqueeze(1).broadcast_to([P, GT, P]),
                                  loc_e[:, bass.ds(local(l, c, CT, g * GT), GT)].unsqueeze(2).broadcast_to([P, GT, P]),
                                  ALU.is_equal)

            def weigh(l, c, g):
                hh = HS[l]
                dve.wait_ge(sm_a, lin(c, SA, 3))
                dve.tensor_tensor(weighted[:, g % 2, :, 0:hh * (F + 1)].rearrange("p t (h f) -> p t h f", h=hh)[:, :, :, 0:F],
                                  rows(l, par(c), g * GT, GT)[:, :, 0:FS[l]].rearrange("p t (h f) -> p t h f", h=hh),
                                  prob_e[:, par(c), g * GT:(g + 1) * GT, 0:hh].unsqueeze(3).broadcast_to([P, GT, hh, F]),
                                  ALU.mult).then_inc(prepared, 1)

            def flush(l, c, t, blk):
                hh = HS[l]
                if t == 0:
                    a = acc[:, bass.ds(blk, 1), 0:hh * (F + 1)].rearrange("p b (h f) -> p (b h) f", h=hh)
                    at_least(dve, flushed, lin(c, CT, 0))
                    dve.tensor_tensor(a, a, rescale[:, 0:hh].unsqueeze(2).broadcast_to([P, hh, F + 1]),
                                      ALU.mult).then_inc(rescaled, 1)
                    dve.wait_ge(rescaled, lin(c, 1, 1))
                a = acc[:, bass.ds(blk, 1), 0:WS[l]].rearrange("p b f -> p (b f)")
                at_least(dve, flushed, lin(c, CT, t))
                dve.wait_ge(summed, lin(c, CT, t + 1))
                dve.tensor_tensor(a, a, ps_o[:, t % 2, 0:WS[l]], ALU.add).then_inc(flushed, 1)

            def run_chunk(l):
                def run(c, scores, soft, plan):
                    for g, before, sums, ahead in plan:
                        if before and sums:
                            blks = blocks_of(dve, l, sums[0], sums[1] * GT - 1, GT)
                        elif sums:
                            blks = (None,) + blocks_of(dve, l, sums[0], sums[1] * GT, GT - 1)
                        elif before:
                            blks = blocks_of(dve, l, before[0], before[1] * GT + GT - 1, 1)
                        if scores and g == 0 and c[0] is None and c[1] == 0:
                            one_hot_t(l, c, 0)
                        if before:
                            flush(l, before[0], before[1] * GT + GT - 1, blks[0])
                        if soft and 0 < g <= 4:
                            softmax(l, shift(c, -1), g - 1)
                        if sums:
                            flush(l, sums[0], sums[1] * GT, blks[1])
                        if scores and g % 2 == 1:
                            one_hot_t(l, c, g // 2 + 1)
                        if ahead:
                            one_hot(l, *ahead)
                        if sums:
                            flush(l, sums[0], sums[1] * GT + 1, blks[2])
                        if ahead:
                            weigh(l, *ahead)
                        if sums:
                            flush(l, sums[0], sums[1] * GT + 2, blks[3])
                return run

            def merge_views(l):
                hh = HS[l]

                def v(k):
                    return small[:, k, :].rearrange("p (b h) -> p b h", b=NB)[:, :, 0:hh]

                return hh, FS[l], v, acc[:, :, 0:hh * (F + 1)].rearrange("p b (h f) -> p b h f", h=hh)

            def merge_weights_of(l):
                hh, fs, v, sums = merge_views(l)
                dve.wait_ge(flushed, (l + 1) * NT)
                l_acc, m_acc, self_ = sums[:, :, :, F], acc[:, :, hh * (F + 1):hh * (F + 2)], s_self[:, :, 0:hh]
                if l == 0 or hh < HMAX:
                    dve.memset(small[:, 2, :], 0.0)
                    link(dve.memset(small[:, 3, :], 0.0))
                link(dve.tensor_scalar(v(0), l_acc, 0.5, -BIG, ALU.is_lt, ALU.mult))
                link(dve.tensor_tensor(v(0), v(0), m_acc, ALU.add))
                link(dve.tensor_tensor(v(1), v(0), self_, ALU.max))
                dve.tensor_tensor(v(2), v(0), v(1), ALU.subtract)
                link(dve.tensor_tensor(v(3), self_, v(1), ALU.subtract))
                dve.sem_inc(merge_ready, 1)
                dve.wait_ge(merge_exp, l + 1)
                link(dve.tensor_tensor(v(4), l_acc, v(2), ALU.mult))
                link(dve.tensor_tensor(v(4), v(4), v(3), ALU.add))
                link(dve.reciprocal(v(5), v(4)))
                dve.tensor_tensor(v(6), v(2), v(5), ALU.mult)
                link(dve.tensor_tensor(v(7), v(3), v(5), ALU.mult))
                dve.sem_inc(merge_weights, 1)

            def merge(l, q):
                hh, fs, v, sums = merge_views(l)
                b0, b1 = STARTS[q], STARTS[q + 1]
                x_sums = sums[:, b0:b1, :, 0:F]
                y = area(0, WR[l])[:, b0:b1, 0:fs]
                xs = y.rearrange("p b (h f) -> p b h f", h=hh)
                h = y if l < NL - 1 else area(1, F)[:, b0:b1, :]
                if q == 0:
                    dve.wait_ge(bias_ready, 16 * (l + 1))
                link(dve.tensor_tensor(x_sums, x_sums, v(6)[:, b0:b1, :].unsqueeze(3).broadcast_to([P, b1 - b0, hh, F]), ALU.mult))
                dve.wait_ge(self_ready, l * MG + q + 1)
                link(dve.tensor_tensor(xs, x_sums, xs, ALU.add))
                link(dve.tensor_tensor(y, y, bias_out[:, 0:fs].unsqueeze(1).broadcast_to([P, b1 - b0, fs]), ALU.add))
                link(dve.scalar_tensor_tensor(out=h, in0=y, scalar=SLOPE_OUT, in1=y, op0=ALU.mult, op1=ALU.max))
                if l < NL - 1:
                    dve.sem_inc(h_ready, 1)

            link(dve.memset(att_bd[:, :, :], 0.0))
            dve.sem_inc(att_room, 1)
            for l in range(NL):
                node_phase(l)
                edge_phase(dve, l, run_chunk(l))
            merge_weights_of(NL - 1)
            for q in range(MG):
                merge(NL - 1, q)

            link(dve.memset(x_place[:, NB - 1:NB, :], 0.0))
            dve.sem_inc(x_again_room, 1)
            dve.wait_ge(x_in, 16 * 6)
            h, sq = area(1, F), area(0, F)

            def over_nodes(v):
                return v.unsqueeze(1).broadcast_to([P, NB, F])

            def over_features(v):
                return v.unsqueeze(2).broadcast_to([P, NB, F])

            def total(q, v):
                link(dve.tensor_reduce(small[:, 0, 0:NB], v, AX.X, ALU.add))
                link(dve.tensor_tensor(small[:, 0, 0:NB], small[:, 0, 0:NB], node_mask[:, :], ALU.mult))
                link(dve.tensor_reduce(tiny[:, q:q + 1], small[:, 0, 0:NB], AX.X, ALU.add))
                dve.sem_inc(stat_ready, 1)
                dve.wait_ge(stat_sum, q + 1)
                link(dve.tensor_scalar(tiny[:, 2 + q:3 + q], ps_m[:, q:q + 1], 1.0 / (N * F), None, ALU.mult))

            def inverse_root(y, v, t, q):
                dve.sem_inc(root_go, 1)
                dve.wait_ge(root_done, q + 1)
                link(dve.reciprocal(y, y_root(q)))
                link(dve.tensor_tensor(t, y, y, ALU.mult))
                link(dve.tensor_tensor(t, t, v, ALU.mult))
                link(dve.tensor_scalar(t, t, -0.5, 1.5, ALU.mult, ALU.add))
                link(dve.tensor_tensor(y, y, t, ALU.mult))

            link(dve.tensor_tensor(h, h, x_place, ALU.add))
            total(0, h)
            link(dve.tensor_scalar(h, h, tiny[:, 2:3], None, ALU.subtract))
            link(dve.tensor_tensor(sq, h, h, ALU.mult))
            total(1, sq)
            link(dve.tensor_scalar(tiny[:, 3:4], tiny[:, 3:4], EPS, None, ALU.add))
            inverse_root(tiny[:, 4:5], tiny[:, 3:4], tiny[:, 5:6], 0)
            link(dve.tensor_scalar(h, h, tiny[:, 4:5], None, ALU.mult))
            link(dve.tensor_tensor(h, h, over_nodes(lnw[:, 0, :]), ALU.mult))
            link(dve.tensor_tensor(h, h, over_nodes(lnw[:, 1, :]), ALU.add))
            link(dve.tensor_tensor(h, h, x_place, ALU.add))
            mean, rstd, var = (small[:, k, 0:NB] for k in range(3))
            link(dve.tensor_reduce(mean, h, AX.X, ALU.add))
            link(dve.tensor_scalar(mean, mean, 1.0 / F, None, ALU.mult))
            link(dve.tensor_tensor(h, h, over_features(mean), ALU.subtract))
            link(dve.tensor_tensor(sq, h, h, ALU.mult))
            link(dve.tensor_reduce(rstd, sq, AX.X, ALU.add))
            link(dve.tensor_scalar(var, rstd, 1.0 / F, EPS, ALU.mult, ALU.add))
            inverse_root(rstd, var, small[:, 3, 0:NB], 1)
            link(dve.tensor_tensor(h, h, over_features(rstd), ALU.mult))
            dve.sem_inc(result_ready, 1)


LAYERS = 4
PART_NAMES = ["Wl", "bl", "Wr", "br", "att", "bias"]


def kernel(**inputs):
    import numpy as np
    import concourse.bacc as bacc
    from concourse import mybir as mb
    from concourse.bass_utils import run_bass_kernel_spmd

    nc = bacc.Bacc("TRN2", target_bir_lowering=False, num_devices=1)
    arrays = {}

    def given(name):
        a = np.ascontiguousarray(inputs[name])
        arrays[f"in_{name}"] = a
        return nc.dram_tensor(f"in_{name}", a.shape, mb.dt.from_np(a.dtype), kind="ExternalInput").ap()

    x, src, dst = (given(n) for n in ("x", "src", "dst"))
    layers = [{n: given(f"L0_gnn_l{l}_{n}") for n in PART_NAMES} for l in range(LAYERS)]
    ln_w, ln_b = given("L0_gnn_ln_w"), given("L0_gnn_ln_b")
    out = nc.dram_tensor("out", x.shape, mb.dt.float32, kind="ExternalOutput").ap()
    program(nc, x, src, dst, layers, ln_w, ln_b, out)
    r = run_bass_kernel_spmd(nc, [arrays], core_ids=[0])
    return r.results[0]["out"]
```
